# Optimizing a Trainium2 kernel written in Bass

```python
import numpy as np
import jax
import jax.numpy as jnp

def _softmax(x, axis=-1):
    return jax.nn.softmax(x, axis=axis)

def _gelu(x):
    return jax.nn.gelu(x, approximate=True)

def _silu(x):
    return jax.nn.silu(x)

def _sigmoid(x):
    return jax.nn.sigmoid(x)

def _layernorm(x, axis=-1, eps=1e-05):
    m = jnp.mean(x, axis=axis, keepdims=True)
    v = jnp.var(x, axis=axis, keepdims=True)
    return (x - m) / jnp.sqrt(v + eps)

def _scatter_add(tgt, idx, src, axis=0):
    return tgt.at[idx].add(src)

def _segment_sum(src, seg, n):
    return jax.ops.segment_sum(src, seg, n)
kernel_name = 'mk_adj_resnorm_d2_adj_r2_100cc3'

def setup_inputs(seed: int=0):
    np.random.seed(seed)
    _w = jnp.asarray

    def _rec_inputs():
        import jax
        import jax.numpy as jnp
        _gk = jax.random.key(seed)
        x = -0.0002928 + 1 * jax.random.normal(jax.random.fold_in(_gk, 1), (8, 1024, 64), jnp.float32)
        _a = jax.random.bernoulli(jax.random.fold_in(_gk, 2), 0.0078125, (1024, 1024))
        _a = jnp.logical_or(_a, jnp.swapaxes(_a, -1, -2))
        _a = jnp.logical_or(_a, jnp.eye(1024, dtype=bool))
        _af = _a.astype(jnp.float32)
        _af = _af * jax.random.uniform(jax.random.fold_in(_gk, 3), (1024, 1024), jnp.float32, 0.05, 0.000488281)
        adj = _af
        return (x, adj)
    x, adj = _rec_inputs()

    def _L0_gnn_setup():
        import jax, jax.numpy as jnp
        import numpy as np
        B, N, IN_SIZE, K, OUT = (32, 1024, 64, 2, 64)
        NUM_MATRICES = 2 * K + 1
        key = jax.random.key(seed)
        k1, k2, k3, k4 = jax.random.split(key, 4)
        inputs_and_state = jax.random.normal(k1, (B, N, IN_SIZE), dtype=jnp.float32)
        support0 = jax.random.uniform(k2, (N, N), dtype=jnp.float32) / N
        support1 = jax.random.uniform(k3, (N, N), dtype=jnp.float32) / N
        fan_in, fan_out = (IN_SIZE * NUM_MATRICES, OUT)
        std = 1.414 * np.sqrt(2.0 / (fan_in + fan_out))
        weight = jax.random.normal(k4, (fan_in, fan_out), dtype=jnp.float32) * std
        bias = jnp.zeros((OUT,), dtype=jnp.float32)
        return {'inputs_and_state': inputs_and_state, 'support0': support0, 'support1': support1, 'weight': weight, 'bias': bias}
    _L0_gnn_all = _L0_gnn_setup()
    _L0_gnn_in = {k: v for k, v in _L0_gnn_all.items() if k in ('weight', 'bias')}
    del _L0_gnn_all

    def _L1_gnn_setup():
        import jax, jax.numpy as jnp
        import numpy as np
        NEG_INF = -1e+16

        def gat_layer(x, graph, W, b):
            h = x @ W
            s = jnp.einsum('bnd,bmd->bnm', h, h) * graph
            s = jnp.where(s == 0.0, NEG_INF, s)
            a = jax.nn.softmax(s, axis=2)
            return jnp.einsum('bnm,bmd->bnd', a, h) + b
        key = jax.random.key(seed)
        k1, k2, k3, k4, k5, k6 = jax.random.split(key, 6)
        B, N, C_IN, HID, HEADS, C_OUT = (16, 512, 64, 128, 8, 64)
        flow_x = jax.random.normal(k1, (B, N, C_IN), dtype=jnp.float32)
        graph = jax.random.randint(k2, (N, N), 0, 2).astype(jnp.float32)
        Wh = jax.random.normal(k3, (HEADS, C_IN, HID), dtype=jnp.float32)
        bh = jax.random.normal(k4, (HEADS, HID), dtype=jnp.float32)
        W_out = jax.random.normal(k5, (HID * HEADS, C_OUT), dtype=jnp.float32)
        b_out = jax.random.normal(k6, (C_OUT,), dtype=jnp.float32)
        return {'flow_x': flow_x, 'graph': graph, 'Wh': Wh, 'bh': bh, 'W_out': W_out, 'b_out': b_out}
    _L1_gnn_all = _L1_gnn_setup()
    _L1_gnn_in = {k: v for k, v in _L1_gnn_all.items() if k in ('Wh', 'bh', 'W_out', 'b_out')}
    del _L1_gnn_all
    return {'x': x, 'adj': adj, 'L0_gnn_weight': _L0_gnn_in['weight'], 'L0_gnn_bias': _L0_gnn_in['bias'], 'L1_gnn_Wh': _L1_gnn_in['Wh'], 'L1_gnn_bh': _L1_gnn_in['bh'], 'L1_gnn_W_out': _L1_gnn_in['W_out'], 'L1_gnn_b_out': _L1_gnn_in['b_out']}

def reference(x, adj, L0_gnn_weight, L0_gnn_bias, L1_gnn_Wh, L1_gnn_bh, L1_gnn_W_out, L1_gnn_b_out):
    import jax
    import jax.numpy as jnp

    def _L0_gnn_ref(inputs_and_state, support0, support1, weight, bias):
        import jax, jax.numpy as jnp
        import numpy as np
        B, N, IN_SIZE, K, OUT = (32, 1024, 64, 2, 64)
        NUM_MATRICES = 2 * K + 1
        x0 = inputs_and_state
        x_stack = [x0]
        for support in (support0, support1):
            x1 = jnp.einsum('ij,bjk->bik', support, x0)
            x_stack.append(x1)
            x_prev, x_curr = (x0, x1)
            for _ in range(2, K + 1):
                x2 = 2.0 * jnp.einsum('ij,bjk->bik', support, x_curr) - x_prev
                x_stack.append(x2)
                x_prev, x_curr = (x_curr, x2)
        x_cat = jnp.concatenate(x_stack, axis=-1)
        out = jnp.einsum('bnf,fo->bno', x_cat, weight) + bias
        return out

    def _L1_gnn_ref(flow_x, graph, Wh, bh, W_out, b_out):
        import jax, jax.numpy as jnp
        import numpy as np
        NEG_INF = -1e+16

        def gat_layer(x, graph, W, b):
            h = x @ W
            s = jnp.einsum('bnd,bmd->bnm', h, h) * graph
            s = jnp.where(s == 0.0, NEG_INF, s)
            a = jax.nn.softmax(s, axis=2)
            return jnp.einsum('bnm,bmd->bnd', a, h) + b
        heads = jax.vmap(lambda W, b: gat_layer(flow_x, graph, W, b))(Wh, bh)
        H, B, N, D = heads.shape
        cat = jnp.moveaxis(heads, 0, 2).reshape(B, N, H * D)
        x = jax.nn.leaky_relu(cat, negative_slope=0.01)
        out = gat_layer(x, graph, W_out, b_out)
        return jax.nn.leaky_relu(out, negative_slope=0.01)
    x = _layernorm(x + _L0_gnn_ref(x, adj, adj, L0_gnn_weight, L0_gnn_bias), axis=-1)
    x = _layernorm(x + _L1_gnn_ref(x, adj, L1_gnn_Wh, L1_gnn_bh, L1_gnn_W_out, L1_gnn_b_out), axis=-1)
    return x

_drawn_inputs = setup_inputs


def setup_inputs(seed=0):
    import zlib

    import numpy as np

    out = dict(_drawn_inputs(seed))
    spreads = {'L0_gnn_bias': (0.0, 0.1)}
    factors = {'L1_gnn_b_out': 7.611}
    for name, (base, spread) in spreads.items():
        noise = np.random.default_rng([zlib.crc32(name.encode()), seed]).standard_normal(out[name].shape)
        drawn = base * np.exp(spread * noise) if base else spread * noise
        out[name] = jnp.asarray(drawn.astype(out[name].dtype))
    for name, factor in factors.items():
        out[name] = (out[name] * factor).astype(out[name].dtype)
    return out
```

```python
from contextlib import ExitStack

import concourse.bass as bass
from concourse import mybir

P = 128
ALU = mybir.AluOpType
ACT = mybir.ActivationFunctionType
F32 = mybir.dt.float32
F32R = mybir.dt.float32r
I32 = mybir.dt.int32
AX_X = mybir.AxisListType.X

NEG_INF = -1e16
NEVER = 1e30
LOWEST = -3e38
SLOPE = 0.01
EPS = 1e-5
BANK = 512


class Job:

    def __init__(self, pair, odd, shift=0):
        n = odd + shift
        self.pair = pair + n // 2
        self.odd = n % 2
        self.at = (pair, odd)

    def back(self, n):
        return Job(self.at[0], self.at[1], -n)

    def count(self, each, plus=0):
        return self.pair * (2 * each) + (self.odd * each + plus)


def wait(eng, sem, value):
    if isinstance(value, int) and value <= 0:
        return
    eng.wait_ge(sem, value)


def program(nc, x, adj, w0, b0, wh, bh, wout, bout, out):
    B, N, C = x.shape
    H, _, D = wh.shape
    NT = N // P
    HT = NT // 2
    JOBS1 = B * H
    JOBS = JOBS1 + B
    assert 2 * C == P and D == P and N == 2 * BANK and H % 2 == 0 and B % 2 == 0

    with ExitStack() as ctx:
        def sb(name, shape, dt=F32, to=ctx):
            return to.enter_context(nc.sbuf_tensor(name, shape, dt))

        def sem(name):
            return ctx.enter_context(nc.semaphore(name))

        x1_dram = nc.dram_tensor("x1_scratch", [B, P, NT * C], F32, kind="Internal").ap()

        graph = sb("graph", [P, NT, N])
        x_hi = sb("x_hi", [P, B, N], F32R)
        x_lo = sb("x_lo", [P, B, N], F32R)
        m_table = sb("m_table", [P, H, P], F32R)
        ident = sb("ident", [P, P])
        dup = sb("dup", [P, C])
        sel = sb("sel", [P, 2, P])
        head_bias = sb("head_bias", [P, H])
        out_bias = sb("out_bias", [P, C])
        general = sb("general", [P, 1], I32)

        prologue(nc, ctx, sem, locals())
        attention(nc, ctx, sem, locals())


def prologue(nc, ctx, sem, env):
    x, adj, w0, b0, wh, bh, bout = (env[k] for k in ("x", "adj", "w0", "b0", "wh", "bh", "bout"))
    B, N, C, H, NT = (env[k] for k in ("B", "N", "C", "H", "NT"))
    graph, x_hi, x_lo, m_table, ident, dup, sel, head_bias, out_bias, general, x1_dram = (
        env[k] for k in ("graph", "x_hi", "x_lo", "m_table", "ident", "dup", "sel", "head_bias", "out_bias",
                         "general", "x1_dram"))
    BC = B * C
    NP = B // 2
    with ExitStack() as tmp:
        def sb(name, shape, dt=F32):
            return tmp.enter_context(nc.sbuf_tensor(name, shape, dt))

        bank = tmp.enter_context(nc.psum_tensor("pro_psum", [P, 8, BANK], F32))
        x0 = sb("x0", [P, NT, BC])
        graph_t = sb("graph_t", [P, NT, N])
        u2 = sb("u2", [P, NT, BC])
        v = sb("v", [P, NT, BC])
        xt = graph_t[:, 0:NP]
        wk = sb("wk", [P, 5, C])
        wbd = sb("wbd", [P, 3, 2, C])
        w_rows = graph_t[0:C, NP].rearrange("c (h d) -> c h d", h=H)
        w_t = graph_t[:, NP + 1].rearrange("p (h k c) -> p h k c", h=H, k=2)
        bias0 = sb("bias0", [P, C])
        resid = sb("resid", [P, 2, B, C])
        cen = sb("cen", [P, 2, B, C])
        sq = sb("sq", [P, 2, B, C])
        x1 = sb("x1", [P, 2, B, 2, C])
        stat = sb("stat", [P, 2, 4, B])
        half = sb("half", [P, B])
        diag = sb("diag", [P, NT])
        dscr = x1[:, 0].rearrange("p b k c -> p b (k c)")
        lows = x1[:, 1, 0, 0, 0:NT]
        bad = sb("bad", [P, 4])
        bias_rows = sb("bias_rows", [H, P])
        badrow = sb("badrow", [1, 1])

        s_ones = sem("p_blank")
        s_adj = [sem(f"p_adj{t}") for t in range(NT)]
        s_x = sem("p_x")
        s_w = sem("p_weights")
        s_id = sem("p_ident")
        s_tr = sem("p_adj_turned")
        s_tc = [sem(f"p_adj_turned_copied{k}") for k in range(2)]
        s_xtr = sem("p_x_turned")
        s_xtc = sem("p_x_turned_copied")
        s_wbd = sem("p_w_combined")
        s_u = sem("p_u")
        s_uc = sem("p_u_copied")
        s_ud = sem("p_u_copied_dve")
        s_own = sem("p_own_part")
        s_av = sem("p_adj_product")
        s_v = sem("p_v")
        s_r = sem("p_resid")
        s_ln = sem("p_norm_dve")
        s_lp = sem("p_norm_pool")
        s_x1 = sem("p_x1")
        s_t1 = sem("p_x1_turned")
        s_hi = sem("p_x1_high")
        s_lo = sem("p_x1_low")
        s_st = [sem(f"p_x1_stored{k}") for k in range(2)]
        s_wtr = sem("p_w_turned")
        s_wtc = sem("p_w_turned_copied")
        s_m = sem("p_m")
        s_mhi = sem("p_m_high")
        s_mlo = sem("p_m_low")
        s_bad = sem("p_bad")
        s_badt = sem("p_bad_turned")
        s_setup = sem("p_setup_dve")

        block = tmp.enter_context(nc.Block())

        @block.sync
        def _(sp):
            for t in range(NT):
                sp.dma_start(graph[:, t, :], adj[t * P:(t + 1) * P, :]).then_inc(s_adj[t], 16)
            for t in range(NT):
                sp.wait_ge(s_x1, t + 1)
                sp.dma_start(x1_dram.rearrange("b p (t c) -> p t b c", c=C)[:, t], x1[:, t % 2, :, 0]).then_inc(s_st[t % 2], 16)
            for k in range(2):
                sp.wait_ge(s_st[k], 16 * (NT // 2))

        @block.scalar
        def _(act):
            for b in range(B):
                act.dma_start(x0[:, :, b * C:(b + 1) * C],
                              x[b].rearrange("(t p) c -> p t c", p=P)).then_inc(s_x, 16)
            for k in range(2):
                act.dma_start(wk[k * C:(k + 1) * C], w0.rearrange("(k c) o -> c k o", c=C)).then_inc(s_w, 16)
            act.dma_start(bias0[:], b0.rearrange("(a c) -> a c", a=1).broadcast_to([P, C])).then_inc(s_w, 16)
            act.dma_start(out_bias[:], bout.rearrange("(a c) -> a c", a=1).broadcast_to([P, C])).then_inc(s_w, 16)
            act.dma_start(w_rows, wh.rearrange("h c d -> c h d")).then_inc(s_w, 16)
            act.dma_start(bias_rows[:], bh).then_inc(s_w, 16)
            for g in range(NT // 2):
                act.wait_ge(s_xtr, g + 1)
                nc.scalar.activation(
                    xt[:, :, 2 * g * P:(2 * g + 2) * P].rearrange("p b (t n) -> p t b n", t=2),
                    bank[:, 4 + 2 * (g % 2):6 + 2 * (g % 2), :].rearrange("p t (b n) -> p t b n", b=NP),
                    ACT.Copy).then_inc(s_xtc, 1)
            act.wait_ge(s_wtr, 1)
            for k in range(2):
                nc.scalar.activation(w_t[:, :, k, :], bank[:, 0, :].rearrange("p (h c) -> p h c", h=H),
                                     ACT.Copy).then_inc(s_wtc, 1)
            nc.scalar.activation(head_bias[:], bank[:, 1, 0:H], ACT.Copy)
            act.wait_ge(s_m, 1)
            nc.scalar.activation(m_table[:], bank[:, 2:4, :].rearrange("p a (h n) -> p (a h) n", n=P),
                                 ACT.Copy).then_inc(s_mhi, 1)
            for t in range(NT):
                act.wait_ge(s_ud, t + 1)
                src = bank[:, 4 * (t % 2):4 * (t % 2) + 4, 0:6 * C].rearrange("p b (k n) -> p b k n", k=3)
                nc.scalar.activation(u2[:, t].rearrange("p (b n) -> p b n", b=NP), src[:, :, 2], ACT.Copy)
                nc.scalar.activation(v[:, t].rearrange("p (b n) -> p b n", b=NP), src[:, :, 1],
                                     ACT.Copy).then_inc(s_uc, 1)
            for t in range(0, NT, 2):
                act.wait_ge(s_tr, t + 1)
                nc.scalar.activation(graph_t[:, :, t * P:(t + 1) * P],
                                     bank[:, 2 * (t % 2):2 * (t % 2) + 2, :].rearrange("p a (j n) -> p (a j) n", n=P),
                                     ACT.Copy).then_inc(s_tc[0], 1)
            for t in range(NT):
                act.wait_ge(s_t1, t + 1)
                nc.scalar.activation(x_hi[:, :, t * P:(t + 1) * P],
                                     bank[:, 4 + 2 * (t % 2):6 + 2 * (t % 2), :].rearrange("p a (b n) -> p (a b) n", n=P),
                                     ACT.Copy).then_inc(s_hi, 1)

        @block.gpsimd
        def _(pool):
            nc.gpsimd.memset(ident[:], 0.0)
            nc.gpsimd.memset(wbd[:], 0.0)
            nc.gpsimd.memset(sel[:], 0.0)
            nc.gpsimd.memset(half[:], -0.5).then_inc(s_ones, 1)
            pool.wait_ge(s_ones, 1)
            nc.gpsimd.affine_select(out=ident[:], in_=ident[:], compare_op=ALU.not_equal, fill=1.0, base=0,
                                    pattern=[[-1, P]], channel_multiplier=1).then_inc(s_id, 1)
            for t in range(NT):
                pool.wait_ge(s_ud, t + 1)
                nc.gpsimd.tensor_tensor(x0[:, t].rearrange("p (b c) -> p b c", b=B),
                                        x0[:, t].rearrange("p (b c) -> p b c", b=B),
                                        bias0[:].rearrange("p (a c) -> p a c", a=1).broadcast_to([P, B, C]),
                                        ALU.add).then_inc(s_own, 1)
            for t in range(NT):
                pool.wait_ge(s_ln, 2 * t + 1)
                nc.gpsimd.tensor_scalar(stat[:, t % 2, 1], stat[:, t % 2, 0], -1.0 / C, 0.0,
                                        ALU.mult, ALU.add).then_inc(s_lp, 1)
                pool.wait_ge(s_ln, 2 * t + 2)
                nc.gpsimd.tensor_scalar(stat[:, t % 2, 3], stat[:, t % 2, 2], 1.0 / C, EPS,
                                        ALU.mult, ALU.add).then_inc(s_lp, 1)
                pool.wait_ge(s_lp, 3 * t + 2)
                nc.gpsimd.tensor_tensor(stat[:, t % 2, 3], stat[:, t % 2, 3], half[:], ALU.pow).then_inc(s_lp, 1)

        @block.vector
        def _(dve):
            dve.wait_ge(s_id, 1)
            nc.vector.tensor_tensor(dup[:], ident[:, 0:C], ident[:, C:P], ALU.add).then_inc(s_setup, 1)
            dve.wait_ge(s_setup, 1)
            for k in range(2):
                rows = slice(k * C, (k + 1) * C)
                nc.vector.tensor_copy(sel[rows, k, 0:C], dup[rows, :]).then_inc(s_setup, 1)
                nc.vector.tensor_copy(sel[rows, k, C:P], dup[rows, :]).then_inc(s_setup, 1)
            dve.wait_ge(s_w, 96)
            for k in range(2):
                rows = slice(k * C, (k + 1) * C)
                for m in (1, 2):
                    nc.vector.tensor_tensor(wbd[rows, m, k, :], wk[rows, m, :], wk[rows, m + 2, :],
                                            ALU.add).then_inc(s_setup, 1)
            dve.wait_ge(s_setup, 9)
            for k in range(2):
                rows = slice(k * C, (k + 1) * C)
                nc.vector.tensor_tensor(wbd[rows, 0, k, :], wk[rows, 0, :], wbd[rows, 2, k, :],
                                        ALU.subtract).then_inc(s_wbd, 1)
            dve.wait_ge(s_mhi, 1)
            nc.vector.tensor_tensor(m_table[C:P], bank[C:P, 2:4, :].rearrange("p a (h n) -> p (a h) n", n=P),
                                    m_table[C:P].bitcast(F32), ALU.subtract).then_inc(s_mlo, 1)
            for t in range(NT):
                dve.wait_ge(s_u, t + 1)
                src = bank[:, 4 * (t % 2):4 * (t % 2) + 4, 0:6 * C].rearrange("p b (k n) -> p b k n", k=3)
                dst = x0[:, t].rearrange("p (b n) -> p b n", b=NP)
                nc.vector.tensor_tensor(dst, src[:, :, 0], dst, ALU.add).then_inc(s_ud, 1)
            for t in range(NT):
                dve.wait_ge(s_adj[t], 16)
                nc.vector.tensor_tensor(dscr[:, t, :], graph[:, t, t * P:(t + 1) * P], ident[:],
                                        ALU.mult).then_inc(s_bad, 1)
            dve.wait_ge(s_bad, NT)
            nc.vector.reduce_sum(diag[:], dscr, AX_X).then_inc(s_bad, 1)
            for t in range(NT):
                nc.vector.tensor_reduce(lows[:, t:t + 1], graph[:, t, :], AX_X, ALU.min).then_inc(s_bad, 1)
            dve.wait_ge(s_bad, 2 * NT + 1)
            nc.vector.tensor_reduce(bad[:, 0:1], lows, AX_X, ALU.min).then_inc(s_bad, 1)
            nc.vector.tensor_reduce(bad[:, 1:2], diag[:], AX_X, ALU.min).then_inc(s_bad, 1)
            dve.wait_ge(s_bad, 2 * NT + 3)
            nc.vector.tensor_scalar(bad[:, 2:3], bad[:, 0:1], 0.0, None, ALU.is_lt).then_inc(s_bad, 1)
            dve.wait_ge(s_bad, 2 * NT + 4)
            nc.vector.scalar_tensor_tensor(out=bad[:, 3:4], in0=bad[:, 1:2], scalar=0.0, in1=bad[:, 2:3],
                                           op0=ALU.is_le, op1=ALU.max).then_inc(s_bad, 1)
            for t in range(1, NT, 2):
                dve.wait_ge(s_tr, t + 1)
                nc.vector.tensor_copy(graph_t[:, :, t * P:(t + 1) * P],
                                      bank[:, 2 * (t % 2):2 * (t % 2) + 2, :].rearrange("p a (j n) -> p (a j) n", n=P)
                                      ).then_inc(s_tc[1], 1)
            for t in range(NT):
                dve.wait_ge(s_av, t + 1)
                nc.vector.scalar_tensor_tensor(out=v[:, t], in0=bank[:, t % 2, :], scalar=2.0, in1=v[:, t],
                                               op0=ALU.mult, op1=ALU.add).then_inc(s_v, 1)
            dve.wait_ge(s_badt, 1)
            nc.vector.tensor_reduce(badrow[:], bank[0:1, 2, 0:P], AX_X, ALU.max).then_inc(s_bad, 1)
            dve.wait_ge(s_bad, 2 * NT + 6)
            nc.vector.tensor_copy(general[0:1, :], badrow[:]).then_inc(s_bad, 1)

            def low_part(t):
                dve.wait_ge(s_hi, t + 1)
                nc.vector.tensor_tensor(x_lo[:, :, t * P:(t + 1) * P],
                                        bank[:, 4 + 2 * (t % 2):6 + 2 * (t % 2), :].rearrange("p a (b n) -> p (a b) n", n=P),
                                        x_hi[:, :, t * P:(t + 1) * P].bitcast(F32), ALU.subtract).then_inc(s_lo, 1)

            for t in range(NT):
                k = t % 2
                dve.wait_ge(s_av, NT + t + 1)
                if t == 0:
                    dve.wait_ge(s_own, NT)
                nc.vector.tensor_tensor(resid[:, k].rearrange("p b c -> p (b c)"), bank[:, t % 2, :], x0[:, t],
                                        ALU.add).then_inc(s_r, 1)
                dve.wait_ge(s_r, 4 * t + 1)
                nc.vector.reduce_sum(stat[:, k, 0], resid[:, k], AX_X).then_inc(s_ln, 1)
                if t >= 1:
                    low_part(t - 1)
                dve.wait_ge(s_lp, 3 * t + 1)
                nc.vector.tensor_tensor(cen[:, k], resid[:, k],
                                        stat[:, k, 1].rearrange("p (b c) -> p b c", c=1).broadcast_to([P, B, C]),
                                        ALU.add).then_inc(s_r, 1)
                dve.wait_ge(s_r, 4 * t + 2)
                nc.vector.tensor_tensor(sq[:, k], cen[:, k], cen[:, k], ALU.mult).then_inc(s_r, 1)
                dve.wait_ge(s_r, 4 * t + 3)
                nc.vector.reduce_sum(stat[:, k, 2], sq[:, k], AX_X).then_inc(s_ln, 1)
                dve.wait_ge(s_lp, 3 * t + 3)
                if t >= 2:
                    dve.wait_ge(s_st[t % 2], 16 * (t // 2))
                    dve.wait_ge(s_t1, t - 1)
                nc.vector.tensor_tensor(x1[:, k], cen[:, k].rearrange("p b (k c) -> p b k c", k=1).broadcast_to([P, B, 2, C]),
                                        stat[:, k, 3].rearrange("p (b k c) -> p b k c", c=1, k=1).broadcast_to([P, B, 2, C]),
                                        ALU.mult).then_inc(s_x1, 1)
                dve.wait_ge(s_x1, t + 1)
                nc.vector.memset(bad[:, 0:1], 0.0).then_inc(s_r, 1)
            low_part(NT - 1)

        @block.tensor
        def _(pe):
            pe.wait_ge(s_id, 1)
            pe.wait_ge(s_w, 96)
            for h in range(H):
                last = nc.tensor.transpose(bank[:, 0, h * C:(h + 1) * C], w_rows[:, h, :], ident[0:C, 0:C])
            nc.tensor.transpose(bank[:, 1, 0:H], bias_rows[:], ident[0:H, 0:H]).then_inc(s_wtr, 1)
            pe.wait_ge(s_x, 16 * B)
            for g in range(NT // 2):
                if g >= 2:
                    pe.wait_ge(s_xtc, g - 1)
                for t in range(2 * g, 2 * g + 2):
                    for b in range(NP):
                        last = nc.tensor.transpose(bank[:, 4 + 2 * (g % 2) + t % 2, b * P:(b + 1) * P],
                                                   x0[:, t, b * P:(b + 1) * P], ident[:])
                last.then_inc(s_xtr, 1)
            pe.wait_ge(s_wtc, 2)
            for h in range(H):
                wt = w_t[:, h].rearrange("p k c -> p (k c)")
                last = nc.tensor.matmul(bank[:, 2 + h // 4, (h % 4) * P:(h % 4 + 1) * P], wt, wt, start=True, stop=True)
            last.then_inc(s_m, 1)
            pe.wait_ge(s_wbd, 2)
            pe.wait_ge(s_xtc, NT // 2)
            pe.wait_ge(s_mlo, 1)
            for t in range(NT):
                if t >= 2:
                    pe.wait_ge(s_uc, t - 1)
                    pe.wait_ge(s_ud, t - 1)
                for b in range(NP):
                    last = nc.tensor.matmul(bank[:, 4 * (t % 2) + b, 0:6 * C], xt[:, b, t * P:(t + 1) * P],
                                            wbd[:].rearrange("p k b c -> p (k b c)"), start=True, stop=True)
                last.then_inc(s_u, 1)
            pe.wait_ge(s_uc, NT)
            pe.wait_ge(s_ud, NT)
            for t in range(NT):
                pe.wait_ge(s_adj[t], 16)
                if t >= 2:
                    pe.wait_ge(s_tc[t % 2], t // 2)
                for j in range(NT):
                    last = nc.tensor.transpose(bank[:, 2 * (t % 2) + j // 4, (j % 4) * P:(j % 4 + 1) * P],
                                               graph[:, t, j * P:(j + 1) * P], ident[:])
                last.then_inc(s_tr, 1)
            for k in range(2):
                pe.wait_ge(s_tc[k], NT // 2)
            for t in range(NT):
                if t >= 2:
                    pe.wait_ge(s_v, t - 1)
                for j in range(NT):
                    last = nc.tensor.matmul(bank[:, t % 2, :], graph_t[:, j, t * P:(t + 1) * P], u2[:, j, :],
                                            start=(j == 0), stop=(j == NT - 1))
                last.then_inc(s_av, 1)
            pe.wait_ge(s_bad, 2 * NT + 5)
            nc.tensor.transpose(bank[0:1, 2, 0:P], bad[:, 3:4], ident[:]).then_inc(s_badt, 1)
            pe.wait_ge(s_v, NT)

            def turn_x1(t):
                pe.wait_ge(s_x1, t + 1)
                if t >= 2:
                    pe.wait_ge(s_lo, t - 1)
                for b in range(B):
                    src = x1[:, t % 2, b].rearrange("p k c -> p (k c)")
                    last = nc.tensor.transpose(bank[:, 4 + 2 * (t % 2) + b // 4, (b % 4) * P:(b % 4 + 1) * P],
                                               src, ident[:])
                last.then_inc(s_t1, 1)

            for t in range(NT):
                if t >= 2:
                    pe.wait_ge(s_r, 4 * (t - 2) + 1)
                for j in range(NT):
                    last = nc.tensor.matmul(bank[:, t % 2, :], graph_t[:, j, t * P:(t + 1) * P], v[:, j, :],
                                            start=(j == 0), stop=(j == NT - 1))
                last.then_inc(s_av, 1)
                if t >= 1:
                    turn_x1(t - 1)
            turn_x1(NT - 1)


def attention(nc, ctx, sem, env):
    wh, wout, out = (env[k] for k in ("wh", "wout", "out"))
    B, N, C, H, D, NT, HT, JOBS1, JOBS = (env[k] for k in ("B", "N", "C", "H", "D", "NT", "HT", "JOBS1", "JOBS"))
    graph, x_hi, x_lo, m_table, ident, dup, sel, head_bias, out_bias, general, x1_dram = (
        env[k] for k in ("graph", "x_hi", "x_lo", "m_table", "ident", "dup", "sel", "head_bias", "out_bias",
                         "general", "x1_dram"))

    def sb(name, shape, dt=F32):
        return ctx.enter_context(nc.sbuf_tensor(name, shape, dt))

    def ps(name, shape):
        return ctx.enter_context(nc.psum_tensor(name, shape, F32))

    scores = ps("scores", [P, 2, N])
    turned = ps("turned", [P, NT, P])
    mixed = ps("mixed", [P, BANK])
    small = ps("small", [P, BANK])

    gated = sb("gated", [P, 2, N])
    prob = sb("prob", [P, 4, N])
    prob_t = sb("prob_t", [P, 2, NT, BANK])
    y_parts = sb("y_parts", [P, 2, N], F32R)
    x_rows = sb("x_rows", [P, 2, NT * C])
    m_now = sb("m_now", [P, 2, P], F32R)
    bias_now = sb("bias_now", [P, 2])
    w_now = sb("w_now", [P, 2, D])
    wout_now = sb("wout_now", [P, 2, C])
    recip_b = sb("recip_b", [P, 2, BANK])
    mixed_n = sb("mixed_n", [P, 2, BANK])
    head_raw = sb("head_raw", [P, 2, BANK])
    head_act = sb("head_act", [P, 2, BANK])
    h_acc = sb("h_acc", [P, B, BANK])
    h_now = sb("h_now", [P, BANK])
    row_max = sb("row_max", [P, NT])
    neg_max = sb("neg_max", [P, NT])
    mask_at = sb("mask_at", [P, NT])
    row_sum = sb("row_sum", [P, 2, NT])
    recip = sb("recip", [P, 2, NT])
    fin, fin2 = (head_raw[:, k].rearrange("p (t c) -> p t c", c=C) for k in range(2))
    x1_b, y_out = (head_act[:, k].rearrange("p (t c) -> p t c", c=C) for k in range(2))
    stat = sb("fstat", [P, 4, NT])
    idle = sb("idle", [P, NT])
    consts = sb("consts", [P, 5, NT])

    s_scores = sem("scores_ready")
    s_gated = sem("gated_ready")
    s_shift = sem("shift_ready")
    s_exp = sem("exp_ready")
    s_prob = sem("prob_ready")
    s_turned = sem("turned_ready")
    s_prob_t = sem("prob_t_ready")
    s_mixed = sem("mixed_ready")
    s_recip = sem("recip_ready")
    s_rb = sem("recip_spread")
    s_rbc = sem("recip_spread_copied")
    s_norm = sem("mixed_n_ready")
    s_post = sem("post_product_ready")
    s_raw = sem("head_raw_ready")
    s_act = sem("head_act_ready")
    s_out1 = sem("wout_product_ready")
    s_acc = sem("h_acc_ready")
    s_zero = sem("h_acc_zeroed")
    s_y = sem("y_product_ready")
    s_yhi = sem("y_high_ready")
    s_ylo = sem("y_low_ready")
    s_hsp = sem("h_parts_spread")
    s_hrow = sem("h_rows_product_ready")
    s_hrc = sem("h_rows_ready")
    s_fin = sem("fin_ready")
    s_fd = sem("final_steps_dve")
    s_fs = sem("final_sums")
    s_fp = sem("final_steps_pool")
    s_m = [sem(f"m_loaded{k}") for k in range(2)]
    s_xr = [sem(f"x_rows_loaded{k}") for k in range(2)]
    s_wl = [sem(f"w_loaded{k}") for k in range(2)]
    s_x1 = sem("x1_b_loaded")
    s_store = sem("out_stored")
    s_consts = sem("consts_ready")
    s_gen = sem("general_dve")

    def kind(n):
        return 0 if n < 0 or n >= JOBS else 1 if n < JOBS1 else 2

    def run(eng, body):
        def one(n):
            body(Job(n // 2, n % 2), kind(n + 1), kind(n), kind(n - 1), kind(n - 2))

        for n in range(2):
            one(n)
        with eng.Fori(1, JOBS1 // 2 - 1) as pair:
            for odd in range(2):
                body(Job(pair, odd), 1, 1, 1, 1)
        for n in range(JOBS1 - 2, JOBS1 + 2):
            one(n)
        with eng.Fori(JOBS1 // 2 + 1, JOBS // 2 - 1) as pair:
            for odd in range(2):
                body(Job(pair, odd), 2, 2, 2, 2)
        for n in range(JOBS - 2, JOBS + 2):
            one(n)

    def batch(job, k):
        return job.pair // (H // 2) if k == 1 else (job.pair - JOBS1 // 2) * 2 + job.odd

    def head(job):
        return (job.pair % (H // 2)) * 2 + job.odd

    block = ctx.enter_context(nc.Block())

    @block.sync
    def _(sp):
        def load_m(job):
            wait(sp, s_y, job.count(2, -2))
            sp.dma_start(m_now[:, job.odd].bitcast(F32), m_table[:, head(job)].bitcast(F32)).then_inc(s_m[job.odd], 16)

        def load_rest(job):
            wait(sp, s_mixed, job.count(2, -2))
            sp.dma_start(x_rows[:, job.odd], x1_dram[batch(job, 1)]).then_inc(s_xr[job.odd], 16)
            wait(sp, s_out1, job.count(1, -1))
            sp.dma_start(bias_now[:, job.odd:job.odd + 1], head_bias[:, bass.ds(head(job), 1)]
                         ).then_inc(s_wl[job.odd], 16)
            for k in range(2):
                sp.dma_start(w_now[k * C:(k + 1) * C, job.odd], wh[head(job)]).then_inc(s_wl[job.odd], 16)
            sp.dma_start(wout_now[:, job.odd], wout.rearrange("(h d) c -> h d c", h=H)[head(job)]
                         ).then_inc(s_wl[job.odd], 16)

        load_m(Job(0, 0))
        for n in range(2):
            load_m(Job(0, n, 1))
            load_rest(Job(0, n))
        with sp.Fori(1, JOBS1 // 2 - 1) as pair:
            for odd in range(2):
                load_m(Job(pair, odd, 1))
                load_rest(Job(pair, odd))
        load_m(Job(JOBS1 // 2 - 1, 1))
        load_rest(Job(JOBS1 // 2 - 1, 0))
        load_rest(Job(JOBS1 // 2 - 1, 1))
        for b in range(B):
            wait(sp, s_fd, 5 * (b - 1) + 2)
            if b == 0:
                sp.wait_ge(s_out1, JOBS1)
            sp.dma_start(x1_b.rearrange("p t c -> p (t c)"), x1_dram[b]).then_inc(s_x1, 16)
            sp.wait_ge(s_fd, 5 * b + 5)
            sp.dma_start(out[b].rearrange("(t p) c -> p t c", p=P), y_out).then_inc(s_store, 16)
        sp.wait_ge(s_store, 16 * B)

    @block.tensor
    def _(pe):
        def y_product(job, k, a, free):
            cols = slice(a * BANK, (a + 1) * BANK)
            b = batch(job, k)
            if k == 1:
                if a == 0:
                    pe.wait_ge(s_m[job.odd], job.pair * 16 + 16)
                nc.tensor.matmul(small[:], m_now[:, job.odd], x_hi[:, b, cols], start=True, stop=False)
                nc.tensor.matmul(small[:], m_now[:, job.odd], x_lo[:, b, cols],
                                 start=False, stop=True).then_inc(s_y, 1)
            else:
                pe.wait_ge(s_acc, b * H + H)
                nc.tensor.matmul(small[:], sel[:, a], h_acc[:, b], start=True, stop=True).then_inc(s_y, 1)

        def post_product(job, k, a):
            pe.wait_ge(s_norm, job.count(2, a + 1))
            if k == 1:
                pe.wait_ge(s_wl[job.odd], job.pair * 64 + 64)
                nc.tensor.matmul(small[:], w_now[:, job.odd], mixed_n[:, a], start=True,
                                 stop=True).then_inc(s_post, 1)
            else:
                for i in range(HT):
                    last = nc.tensor.matmul(small[:, i * C:(i + 1) * C], mixed_n[:, a, i * P:(i + 1) * P],
                                            dup[:], start=True, stop=True)
                last.then_inc(s_post, 1)

        def spread_recip(job, a):
            pe.wait_ge(s_recip, job.count(2, a + 1))
            for i in range(HT):
                src = recip[:, job.odd, a * HT + i:a * HT + i + 1].broadcast_to([P, P])
                last = nc.tensor.transpose(small[:, i * P:(i + 1) * P], src, ident[:])
            last.then_inc(s_rb, 1)

        def post_free(job, k, a):
            if k == 1:
                wait(pe, s_raw, job.count(2, a + 1))
            elif k == 2:
                pe.wait_ge(s_fin, job.count(2, a + 1 - 2 * JOBS1))

        def body(job, nxt, now, bef, bef2):
            j1, j2, jn = job.back(1), job.back(2), job.back(-1)
            for t in range(NT):
                if now:
                    wait(pe, s_gated, job.count(NT, t - 1))
                    if t == 0:
                        pe.wait_ge(s_ylo, job.count(2, 2))
                    b = batch(job, now)
                    for a in range(2):
                        cols = slice(a * BANK, (a + 1) * BANK)
                        lhs = y_parts[:, job.odd, t * P:(t + 1) * P]
                        nc.tensor.matmul(scores[:, t % 2, cols], lhs, x_hi[:, b, cols], start=True, stop=False)
                        last = nc.tensor.matmul(scores[:, t % 2, cols], lhs, x_lo[:, b, cols], start=False, stop=True)
                    last.then_inc(s_scores, 1)
                if bef:
                    a, pair = t // HT, t % HT
                    if pair == 0:
                        pe.wait_ge(s_prob_t, j1.count(NT, a * HT + HT))
                        wait(pe, s_norm, j1.count(2, a))
                    if t == 0:
                        if bef == 1:
                            pe.wait_ge(s_xr[j1.odd], j1.pair * 16 + 16)
                        else:
                            pe.wait_ge(s_hrc, j1.count(1, 1 - JOBS1))
                    for e in range(2):
                        m = 2 * pair + e
                        last = nc.tensor.matmul(mixed[e * C:(e + 1) * C, :], x_rows[:, j1.odd, m * C:(m + 1) * C],
                                                prob_t[:, a, m, :], start=(pair == 0), stop=(pair == HT - 1))
                    if pair == HT - 1:
                        last.then_inc(s_mixed, 1)
                if (t >= 3 and now) or (t < 3 and bef):
                    pe.wait_ge(s_prob, job.count(NT, t - 2))
                    wait(pe, s_prob_t, job.count(NT, t - 3))
                    for m in range(NT):
                        last = nc.tensor.transpose(turned[:, m, :], prob[:, (t - 3) % 4, m * P:(m + 1) * P], ident[:])
                    last.then_inc(s_turned, 1)
                if t == 1 and bef2:
                    post_free(j2, bef2, 0)
                    post_product(j2, bef2, 1)
                if t == 2 and bef:
                    post_free(j2, bef2, 1)
                    if not bef2:
                        pe.wait_ge(s_ylo, 2 * 2)
                    spread_recip(j1, 0)
                if t == 3 and bef2 == 1:
                    wait(pe, s_rbc, j1.count(2, 1) if bef else 0)
                    pe.wait_ge(s_act, j2.count(2, 2))
                    for a in range(2):
                        last = nc.tensor.matmul(small[a * C:(a + 1) * C, :], wout_now[:, j2.odd], head_act[:, a],
                                                start=True, stop=True)
                    last.then_inc(s_out1, 1)
                if t == 3 and now == 2:
                    pe.wait_ge(s_rbc, j1.count(2, 1))
                    if bef2 == 1:
                        pe.wait_ge(s_acc, j2.count(1, 1))
                    for i in range(HT):
                        last = nc.tensor.transpose(small[:, i * P:(i + 1) * P], h_now[:, i * P:(i + 1) * P], ident[:])
                    last.then_inc(s_hrow, 1)
                if t == 4 and bef:
                    pe.wait_ge(s_rbc, j1.count(2, 1))
                    if bef2 == 1:
                        pe.wait_ge(s_acc, j2.count(1, 1))
                    if now == 2:
                        pe.wait_ge(s_hrc, job.count(1, 1 - JOBS1))
                    spread_recip(j1, 1)
                if t in (5, 6) and nxt:
                    if t == 5 and bef:
                        pe.wait_ge(s_rbc, j1.count(2, 2))
                    wait(pe, s_ylo, jn.count(2, t - 5))
                    y_product(jn, nxt, t - 5, None)
                if t == 7 and bef:
                    if nxt:
                        pe.wait_ge(s_ylo, jn.count(2, 2))
                    pe.wait_ge(s_rbc, j1.count(2, 2))
                    post_product(j1, bef, 0)

        y_product(Job(0, 0), 1, 0, None)
        pe.wait_ge(s_ylo, 1)
        y_product(Job(0, 0), 1, 1, None)
        run(pe, body)

    @block.scalar
    def _(act):
        def y_high(job, k, a):
            cols = slice(a * BANK, (a + 1) * BANK)
            act.wait_ge(s_y, job.count(2, a + 1))
            if k == 2:
                wait(act, s_hrow, job.count(1, -JOBS1))
                rows = slice(a * C, (a + 1) * C)
                nc.scalar.activation(h_now[rows, :], small[rows, :], ACT.Copy)
            nc.scalar.activation(y_parts[:, job.odd, cols], small[:], ACT.Copy).then_inc(s_yhi, 1)

        def copy_recip(job, a):
            act.wait_ge(s_rb, job.count(2, a + 1))
            wait(act, s_norm, job.count(2, a - 1))
            nc.scalar.activation(recip_b[:, a], small[:], ACT.Copy).then_inc(s_rbc, 1)

        def head_out(job, a):
            act.wait_ge(s_post, job.count(2, a + 1))
            wait(act, s_act, job.count(2, a - 1))
            nc.scalar.activation(head_raw[:, a], small[:], ACT.Identity, bias=bias_now[:, job.odd:job.odd + 1],
                                 scale=1.0).then_inc(s_raw, 1)

        def body(job, nxt, now, bef, bef2):
            j1, j2, jn = job.back(1), job.back(2), job.back(-1)
            for t in range(NT):
                if (t >= 1 and now) or (t < 1 and bef):
                    act.wait_ge(s_shift, job.count(NT, t))
                    wait(act, s_turned, job.count(NT, t - 4))
                    k = (t - 1) % NT
                    nc.scalar.activation(prob[:, k % 4], gated[:, k % 2], ACT.Exp, bias=neg_max[:, k:k + 1],
                                         scale=1.0).then_inc(s_exp, 1)
                if (t >= 3 and now) or (t < 3 and bef):
                    k = (t - 3) % NT
                    act.wait_ge(s_turned, job.count(NT, t - 2))
                    if k % HT == 0:
                        wait(act, s_mixed, (job if t >= 3 else j1).count(2, k // HT - 1))
                    nc.scalar.activation(prob_t[:, k // HT, :, (k % HT) * P:(k % HT + 1) * P], turned[:],
                                         ACT.Copy).then_inc(s_prob_t, 1)
                if t == 1 and bef2 == 1:
                    head_out(j2, 1)
                if t == 2 and bef:
                    copy_recip(j1, 0)
                if t == 3 and now == 2:
                    act.wait_ge(s_hrow, job.count(1, 1 - JOBS1))
                    act.wait_ge(s_mixed, job.count(2, -2))
                    nc.scalar.activation(x_rows[:, job.odd].rearrange("p (a i c) -> p i a c", a=2, c=C),
                                         small[:].rearrange("p (i a c) -> p i a c", a=2, c=C),
                                         ACT.Copy).then_inc(s_hrc, 1)
                if t == 4 and bef:
                    copy_recip(j1, 1)
                if t in (5, 6) and nxt:
                    y_high(jn, nxt, t - 5)
                if t == 7 and bef == 1:
                    head_out(j1, 0)

        for a in range(2):
            y_high(Job(0, 0), 1, a)
        run(act, body)

    @block.gpsimd
    def _(pool):
        for k, value in enumerate((-1.0, -0.5, -1.0 / C, 1.0 / C, EPS)):
            nc.gpsimd.memset(consts[:, k], value).then_inc(s_consts, 1)
        pool.wait_ge(s_consts, 5)

        def body(job, nxt, now, bef, bef2):
            j1, j2, jn = job.back(1), job.back(2), job.back(-1)
            for t in range(NT):
                if now:
                    pool.wait_ge(s_gated, job.count(NT, t + 1))
                    nc.gpsimd.tensor_tensor(neg_max[:, t:t + 1], row_max[:, t:t + 1], consts[:, 0, 0:1], ALU.mult)
                    nc.gpsimd.tensor_scalar(mask_at[:, t:t + 1], row_max[:, t:t + 1], 0.0, NEVER, ALU.is_le,
                                            ALU.mult).then_inc(s_shift, 1)
                if bef2 == 2 and t == 3:
                    pool.wait_ge(s_fs, j2.count(2, 1 - 2 * JOBS1))
                    nc.gpsimd.tensor_tensor(stat[:, 1], stat[:, 0], consts[:, 2], ALU.mult).then_inc(s_fp, 1)
                if bef2 == 2 and t == 4:
                    pool.wait_ge(s_fs, j2.count(2, 2 - 2 * JOBS1))
                    nc.gpsimd.tensor_tensor(stat[:, 3], stat[:, 2], consts[:, 3], ALU.mult).then_inc(s_fp, 1)
                    pool.wait_ge(s_fp, j2.count(4, 2 - 4 * JOBS1))
                    nc.gpsimd.tensor_tensor(stat[:, 3], stat[:, 3], consts[:, 4], ALU.add).then_inc(s_fp, 1)
                    pool.wait_ge(s_fp, j2.count(4, 3 - 4 * JOBS1))
                    nc.gpsimd.tensor_tensor(stat[:, 3], stat[:, 3], consts[:, 1], ALU.pow).then_inc(s_fp, 1)

        run(pool, body)

    @block.vector
    def _(dve):
        def y_low(job, k, a):
            cols = slice(a * BANK, (a + 1) * BANK)
            dve.wait_ge(s_yhi, job.count(2, a + 1))
            if k == 2:
                n = job.count(4, 2 * a - 4 * JOBS1)
                nc.vector.tensor_scalar(x_hi[:, batch(job, 2), cols], y_parts[:, job.odd, cols].bitcast(F32), 1.0, None,
                                        ALU.mult).then_inc(s_hsp, 1)
                nc.vector.tensor_tensor(x_lo[:, batch(job, 2), cols], small[:],
                                        y_parts[:, job.odd, cols].bitcast(F32), ALU.subtract).then_inc(s_hsp, 1)
                dve.wait_ge(s_hsp, n + 2)
            nc.vector.tensor_tensor(y_parts[C:P, job.odd, cols], small[C:P, :],
                                    y_parts[C:P, job.odd, cols].bitcast(F32), ALU.subtract).then_inc(s_ylo, 1)

        def reciprocals(job, a):
            dve.wait_ge(s_prob, job.count(NT, a * HT + HT))
            wait(dve, s_rb, job.count(2, a - 3))
            cols = slice(a * HT, (a + 1) * HT)
            nc.vector.reciprocal(recip[:, job.odd, cols], row_sum[:, job.odd, cols]).then_inc(s_recip, 1)

        def normalise(job, a):
            dve.wait_ge(s_mixed, job.count(2, a + 1))
            dve.wait_ge(s_rbc, job.count(2, a + 1))
            wait(dve, s_post, job.count(2, a - 1))
            nc.vector.tensor_tensor(mixed_n[:, a], mixed[:], recip_b[:, a], ALU.mult).then_inc(s_norm, 1)

        def leaky(job, a):
            dve.wait_ge(s_raw, job.count(2, a + 1))
            wait(dve, s_out1, job.count(1, 0))
            nc.vector.scalar_tensor_tensor(out=head_act[:, a], in0=head_raw[:, a], scalar=SLOPE, in1=head_raw[:, a],
                                           op0=ALU.mult, op1=ALU.max).then_inc(s_act, 1)

        def accumulate(job):
            dve.wait_ge(s_out1, job.count(1, 1))
            wait(dve, s_acc, job.count(1, 0))
            b = batch(job, 1)
            nc.vector.tensor_tensor(h_acc[:, b], small[:], h_acc[:, b], ALU.add).then_inc(s_acc, 1)

        def final_rows(job, a):
            dve.wait_ge(s_post, job.count(2, a + 1))
            if isinstance(job.pair, int):
                wait(dve, s_fd, job.count(5, 1 - 5 * JOBS1 - 5))
            else:
                dve.wait_ge(s_gated, job.count(NT, 2 * NT))
            nc.vector.tensor_tensor(fin[:, a * HT:(a + 1) * HT, :],
                                    small[:, 0:HT * C].rearrange("p (t c) -> p t c", c=C),
                                    out_bias[:].rearrange("p (a c) -> p a c", a=1).broadcast_to([P, HT, C]),
                                    ALU.add).then_inc(s_fin, 1)

        def spread(row):
            return row.rearrange("p (t c) -> p t c", c=1).broadcast_to([P, NT, C])

        def final_steps(job, part):
            n = job.count(1, -JOBS1)
            if part == 0:
                dve.wait_ge(s_fin, n * 2 + 2)
                wait(dve, s_fd, n * 5)
                nc.vector.scalar_tensor_tensor(out=fin2, in0=fin, scalar=SLOPE, in1=fin, op0=ALU.mult,
                                               op1=ALU.max).then_inc(s_fd, 1)
                dve.wait_ge(s_fd, n * 5 + 1)
                dve.wait_ge(s_x1, n * 16 + 16)
                nc.vector.tensor_tensor(fin2, fin2, x1_b, ALU.add).then_inc(s_fd, 1)
                dve.wait_ge(s_fd, n * 5 + 2)
                nc.vector.reduce_sum(stat[:, 0], fin2, AX_X).then_inc(s_fs, 1)
            elif part == 1:
                dve.wait_ge(s_fp, n * 4 + 1)
                dve.wait_ge(s_fs, n * 2 + 1)
                nc.vector.tensor_tensor(fin2, fin2, spread(stat[:, 1]), ALU.add).then_inc(s_fd, 1)
                dve.wait_ge(s_fd, n * 5 + 3)
                wait(dve, s_store, n * 16)
                nc.vector.tensor_tensor(y_out, fin2, fin2, ALU.mult).then_inc(s_fd, 1)
                dve.wait_ge(s_fd, n * 5 + 4)
                nc.vector.reduce_sum(stat[:, 2], y_out, AX_X).then_inc(s_fs, 1)
            else:
                dve.wait_ge(s_fp, n * 4 + 4)
                dve.wait_ge(s_fs, n * 2 + 2)
                nc.vector.tensor_tensor(y_out, fin2, spread(stat[:, 3]), ALU.mult).then_inc(s_fd, 1)

        def pipeline(general_graph):
            def body(job, nxt, now, bef, bef2):
                j1, j2, jn = job.back(1), job.back(2), job.back(-1)
                for t in range(NT):
                    if t == 0 and bef2:
                        normalise(j2, 1)
                        if bef2 == 1:
                            leaky(j2, 0)
                        else:
                            final_rows(j2, 0)
                    if t == 2 and bef:
                        reciprocals(j1, 1)
                    if t == 2 and bef2 == 1:
                        leaky(j2, 1)
                    if t == 2 and bef2 == 2:
                        final_rows(j2, 1)
                    if t == 3 and bef2 == 2:
                        final_steps(j2, 0)
                    if t == 4 and bef2 == 1:
                        accumulate(j2)
                    if t == 4 and bef2 == 2:
                        final_steps(j2, 1)
                    if t == 4 and bef:
                        normalise(j1, 0)
                    if t == 6 and now:
                        reciprocals(job, 0)
                    if t in (6, 7) and nxt:
                        y_low(jn, nxt, t - 6)
                    if t == 6 and bef2 == 2:
                        final_steps(j2, 2)
                    if (t >= 2 and now) or (t < 2 and bef):
                        k = (t - 2) % NT
                        dve.wait_ge(s_exp, job.count(NT, t - 1))
                        nc.vector.scalar_tensor_tensor(
                            out=prob[:, k % 4], in0=gated[:, k % 2], scalar=mask_at[:, k:k + 1], in1=prob[:, k % 4],
                            op0=ALU.not_equal, op1=ALU.mult,
                            accum_out=row_sum[:, (job if t >= 2 else j1).odd, k:k + 1]).then_inc(s_prob, 1)
                    if now:
                        n = job.count(2 * NT, 2 * t)
                        dve.wait_ge(s_scores, job.count(NT, t + 1))
                        wait(dve, s_prob, job.count(NT, t - 1))
                        nc.vector.memset(idle[:, t:t + 1], 0.0)
                        ins = nc.vector.tensor_tensor_reduce(
                            out=gated[:, t % 2], in0=scores[:, t % 2], in1=graph[:, t], scale=1.0, scalar=LOWEST,
                            op0=ALU.mult, op1=ALU.max, accum_out=row_max[:, t:t + 1])
                        if not general_graph:
                            ins.then_inc(s_gated, 1)
                        else:
                            ins.then_inc(s_gen, 1)
                            dve.wait_ge(s_gen, n + 1)
                            zeros = prob[:, t % 4]
                            nc.vector.tensor_scalar(zeros, gated[:, t % 2], 0.0, NEG_INF, ALU.is_equal,
                                                    ALU.mult).then_inc(s_gen, 1)
                            dve.wait_ge(s_gen, n + 2)
                            nc.vector.memset(idle[:, t:t + 1], 0.0)
                            nc.vector.tensor_tensor_reduce(
                                out=gated[:, t % 2], in0=gated[:, t % 2], in1=zeros, scale=1.0, scalar=LOWEST,
                                op0=ALU.add, op1=ALU.max, accum_out=row_max[:, t:t + 1]).then_inc(s_gated, 1)

            for a in range(2):
                y_low(Job(0, 0), 1, a)
            run(dve, body)

        nc.vector.memset(h_acc[:], 0.0).then_inc(s_zero, 1)
        dve.wait_ge(s_zero, 1)
        flag = dve.value_load(general[0:1, 0:1], min_val=0, max_val=1)
        with dve.If(flag == 0):
            pipeline(False)
        with dve.Else():
            pipeline(True)


_INS = ['x', 'adj', 'L0_gnn_weight', 'L0_gnn_bias', 'L1_gnn_Wh', 'L1_gnn_bh', 'L1_gnn_W_out', 'L1_gnn_b_out']


def kernel(**inputs):
    import numpy as _np
    import concourse.bacc as _bacc
    from concourse import mybir as _mybir
    from concourse.bass_utils import run_bass_kernel_spmd as _run

    nc = _bacc.Bacc("TRN2", target_bir_lowering=False, num_devices=1)
    arrays, args = {}, []
    for name in _INS:
        a = _np.ascontiguousarray(inputs[name])
        arrays[f"in_{name}"] = a
        args.append(nc.dram_tensor(f"in_{name}", a.shape, _mybir.dt.from_np(a.dtype), kind="ExternalInput").ap())
    args.append(nc.dram_tensor("out_0", inputs['x'].shape, _mybir.dt.float32, kind="ExternalOutput").ap())
    program(nc, *args)
    r = _run(nc, [arrays], core_ids=[0])
    return r.results[0]["out_0"]
```

```python
from contextlib import ExitStack

import concourse.bass as bass
from concourse import mybir

P = 128
ALU = mybir.AluOpType
ACT = mybir.ActivationFunctionType
F32 = mybir.dt.float32
F32R = mybir.dt.float32r
I32 = mybir.dt.int32
AX_X = mybir.AxisListType.X

NEG_INF = -1e16
NEVER = 1e30
LOWEST = -3e38
SLOPE = 0.01
EPS = 1e-5
BANK = 512


class Job:

    def __init__(self, pair, odd, shift=0):
        n = odd + shift
        self.pair = pair + n // 2
        self.odd = n % 2
        self.at = (pair, odd)

    def back(self, n):
        return Job(self.at[0], self.at[1], -n)

    def count(self, each, plus=0):
        return self.pair * (2 * each) + (self.odd * each + plus)


def wait(eng, sem, value):
    if isinstance(value, int) and value <= 0:
        return
    eng.wait_ge(sem, value)


def program(nc, x, adj, w0, b0, wh, bh, wout, bout, out):
    B, N, C = x.shape
    H, _, D = wh.shape
    NT = N // P
    HT = NT // 2
    JOBS1 = B * H
    JOBS = JOBS1 + B
    assert 2 * C == P and D == P and N == 2 * BANK and H % 2 == 0 and B % 2 == 0

    with ExitStack() as ctx:
        def sb(name, shape, dt=F32, to=ctx):
            return to.enter_context(nc.sbuf_tensor(name, shape, dt))

        def sem(name):
            return ctx.enter_context(nc.semaphore(name))

        x1_dram = nc.dram_tensor("x1_scratch", [B, P, NT * C], F32, kind="Internal").ap()

        graph = sb("graph", [P, NT, N])
        x_hi = sb("x_hi", [P, B, N], F32R)
        x_lo = sb("x_lo", [P, B, N], F32R)
        m_table = sb("m_table", [P, H, P], F32R)
        ident = sb("ident", [P, P])
        dup = sb("dup", [P, C])
        sel = sb("sel", [P, 2, P])
        head_bias = sb("head_bias", [P, H, 2])
        out_bias = sb("out_bias", [P, C])
        general = sb("general", [P, 1], I32)

        prologue(nc, ctx, sem, locals())
        attention(nc, ctx, sem, locals())


def prologue(nc, ctx, sem, env):
    x, adj, w0, b0, wh, bh, bout = (env[k] for k in ("x", "adj", "w0", "b0", "wh", "bh", "bout"))
    B, N, C, H, NT = (env[k] for k in ("B", "N", "C", "H", "NT"))
    graph, x_hi, x_lo, m_table, ident, dup, sel, head_bias, out_bias, general, x1_dram = (
        env[k] for k in ("graph", "x_hi", "x_lo", "m_table", "ident", "dup", "sel", "head_bias", "out_bias",
                         "general", "x1_dram"))
    BC = B * C
    NP = B // 2
    with ExitStack() as tmp:
        def sb(name, shape, dt=F32):
            return tmp.enter_context(nc.sbuf_tensor(name, shape, dt))

        bank = tmp.enter_context(nc.psum_tensor("pro_psum", [P, 8, BANK], F32))
        x0 = sb("x0", [P, NT, BC])
        graph_t = sb("graph_t", [P, NT, N])
        u2 = sb("u2", [P, NT, BC])
        v = sb("v", [P, NT, BC])
        xt = graph_t[:, 0:NP]
        wk = sb("wk", [P, 5, C])
        wbd = sb("wbd", [P, 3, 2, C])
        w_rows = graph_t[0:C, NP].rearrange("c (h d) -> c h d", h=H)
        w_t = graph_t[:, NP + 1].rearrange("p (h k c) -> p h k c", h=H, k=2)
        bias0 = sb("bias0", [P, C])
        resid = sb("resid", [P, 2, B, C])
        cen = sb("cen", [P, 2, B, C])
        sq = sb("sq", [P, 2, B, C])
        x1 = sb("x1", [P, 2, B, 2, C])
        stat = sb("stat", [P, 2, 4, B])
        half = sb("half", [P, B])
        diag = sb("diag", [P, NT])
        dscr = x1[:, 0].rearrange("p b k c -> p b (k c)")
        lows = x1[:, 1, 0, 0, 0:NT]
        bad = sb("bad", [P, 4])
        bias_rows = sb("bias_rows", [H, P])
        badrow = sb("badrow", [1, 1])

        s_ones = sem("p_blank")
        s_adj = [sem(f"p_adj{t}") for t in range(NT)]
        s_x = sem("p_x")
        s_w = sem("p_weights")
        s_id = sem("p_ident")
        s_tr = sem("p_adj_turned")
        s_tc = [sem(f"p_adj_turned_copied{k}") for k in range(2)]
        s_xtr = sem("p_x_turned")
        s_xtc = sem("p_x_turned_copied")
        s_wbd = sem("p_w_combined")
        s_u = sem("p_u")
        s_uc = sem("p_u_copied")
        s_ud = sem("p_u_copied_dve")
        s_own = sem("p_own_part")
        s_av = sem("p_adj_product")
        s_v = sem("p_v")
        s_r = sem("p_resid")
        s_ln = sem("p_norm_dve")
        s_lp = sem("p_norm_pool")
        s_x1 = sem("p_x1")
        s_t1 = sem("p_x1_turned")
        s_hi = sem("p_x1_high")
        s_lo = sem("p_x1_low")
        s_st = [sem(f"p_x1_stored{k}") for k in range(2)]
        s_wtr = sem("p_w_turned")
        s_wtc = sem("p_w_turned_copied")
        s_m = sem("p_m")
        s_mhi = sem("p_m_high")
        s_mlo = sem("p_m_low")
        s_bad = sem("p_bad")
        s_badt = sem("p_bad_turned")
        s_setup = sem("p_setup_dve")

        block = tmp.enter_context(nc.Block())

        @block.sync
        def _(sp):
            for t in range(NT):
                sp.dma_start(graph[:, t, :], adj[t * P:(t + 1) * P, :]).then_inc(s_adj[t], 16)
            for t in range(NT):
                sp.wait_ge(s_x1, t + 1)
                sp.dma_start(x1_dram.rearrange("b p (t c) -> p t b c", c=C)[:, t], x1[:, t % 2, :, 0]).then_inc(s_st[t % 2], 16)
            for k in range(2):
                sp.wait_ge(s_st[k], 16 * (NT // 2))

        @block.scalar
        def _(act):
            for b in range(B):
                act.dma_start(x0[:, :, b * C:(b + 1) * C],
                              x[b].rearrange("(t p) c -> p t c", p=P)).then_inc(s_x, 16)
            for k in range(2):
                act.dma_start(wk[k * C:(k + 1) * C], w0.rearrange("(k c) o -> c k o", c=C)).then_inc(s_w, 16)
            act.dma_start(bias0[:], b0.rearrange("(a c) -> a c", a=1).broadcast_to([P, C])).then_inc(s_w, 16)
            act.dma_start(out_bias[:], bout.rearrange("(a c) -> a c", a=1).broadcast_to([P, C])).then_inc(s_w, 16)
            act.dma_start(w_rows, wh.rearrange("h c d -> c h d")).then_inc(s_w, 16)
            act.dma_start(bias_rows[:], bh).then_inc(s_w, 16)
            for g in range(NT // 2):
                act.wait_ge(s_xtr, g + 1)
                nc.scalar.activation(
                    xt[:, :, 2 * g * P:(2 * g + 2) * P].rearrange("p b (t n) -> p t b n", t=2),
                    bank[:, 4 + 2 * (g % 2):6 + 2 * (g % 2), :].rearrange("p t (b n) -> p t b n", b=NP),
                    ACT.Copy).then_inc(s_xtc, 1)
            act.wait_ge(s_wtr, 1)
            for k in range(2):
                nc.scalar.activation(w_t[:, :, k, :], bank[:, 0, :].rearrange("p (h c) -> p h c", h=H),
                                     ACT.Copy).then_inc(s_wtc, 1)
            for k, factor in enumerate((1.0, -SLOPE)):
                nc.scalar.activation(head_bias[:, :, k], bank[:, 1, 0:H], ACT.Copy, scale=factor)
            act.wait_ge(s_m, 1)
            nc.scalar.activation(m_table[:], bank[:, 2:4, :].rearrange("p a (h n) -> p (a h) n", n=P),
                                 ACT.Copy).then_inc(s_mhi, 1)
            for t in range(NT):
                act.wait_ge(s_ud, t + 1)
                src = bank[:, 4 * (t % 2):4 * (t % 2) + 4, 0:6 * C].rearrange("p b (k n) -> p b k n", k=3)
                nc.scalar.activation(u2[:, t].rearrange("p (b n) -> p b n", b=NP), src[:, :, 2], ACT.Copy)
                nc.scalar.activation(v[:, t].rearrange("p (b n) -> p b n", b=NP), src[:, :, 1],
                                     ACT.Copy).then_inc(s_uc, 1)
            for t in range(0, NT, 2):
                act.wait_ge(s_tr, t + 1)
                nc.scalar.activation(graph_t[:, :, t * P:(t + 1) * P],
                                     bank[:, 2 * (t % 2):2 * (t % 2) + 2, :].rearrange("p a (j n) -> p (a j) n", n=P),
                                     ACT.Copy).then_inc(s_tc[0], 1)
            for t in range(NT):
                act.wait_ge(s_t1, t + 1)
                nc.scalar.activation(x_hi[:, :, t * P:(t + 1) * P],
                                     bank[:, 4 + 2 * (t % 2):6 + 2 * (t % 2), :].rearrange("p a (b n) -> p (a b) n", n=P),
                                     ACT.Copy).then_inc(s_hi, 1)

        @block.gpsimd
        def _(pool):
            nc.gpsimd.memset(ident[:], 0.0)
            nc.gpsimd.memset(wbd[:], 0.0)
            nc.gpsimd.memset(sel[:], 0.0)
            nc.gpsimd.memset(half[:], -0.5).then_inc(s_ones, 1)
            pool.wait_ge(s_ones, 1)
            nc.gpsimd.affine_select(out=ident[:], in_=ident[:], compare_op=ALU.not_equal, fill=1.0, base=0,
                                    pattern=[[-1, P]], channel_multiplier=1).then_inc(s_id, 1)
            for t in range(NT):
                pool.wait_ge(s_ud, t + 1)
                nc.gpsimd.tensor_tensor(x0[:, t].rearrange("p (b c) -> p b c", b=B),
                                        x0[:, t].rearrange("p (b c) -> p b c", b=B),
                                        bias0[:].rearrange("p (a c) -> p a c", a=1).broadcast_to([P, B, C]),
                                        ALU.add).then_inc(s_own, 1)
            for t in range(NT):
                pool.wait_ge(s_ln, 2 * t + 1)
                nc.gpsimd.tensor_scalar(stat[:, t % 2, 1], stat[:, t % 2, 0], -1.0 / C, 0.0,
                                        ALU.mult, ALU.add).then_inc(s_lp, 1)
                pool.wait_ge(s_ln, 2 * t + 2)
                nc.gpsimd.tensor_scalar(stat[:, t % 2, 3], stat[:, t % 2, 2], 1.0 / C, EPS,
                                        ALU.mult, ALU.add).then_inc(s_lp, 1)
                pool.wait_ge(s_lp, 3 * t + 2)
                nc.gpsimd.tensor_tensor(stat[:, t % 2, 3], stat[:, t % 2, 3], half[:], ALU.pow).then_inc(s_lp, 1)

        @block.vector
        def _(dve):
            dve.wait_ge(s_id, 1)
            nc.vector.tensor_tensor(dup[:], ident[:, 0:C], ident[:, C:P], ALU.add).then_inc(s_setup, 1)
            dve.wait_ge(s_setup, 1)
            for k in range(2):
                rows = slice(k * C, (k + 1) * C)
                nc.vector.tensor_copy(sel[rows, k, 0:C], dup[rows, :]).then_inc(s_setup, 1)
                nc.vector.tensor_copy(sel[rows, k, C:P], dup[rows, :]).then_inc(s_setup, 1)
            dve.wait_ge(s_w, 96)
            for k in range(2):
                rows = slice(k * C, (k + 1) * C)
                for m in (1, 2):
                    nc.vector.tensor_tensor(wbd[rows, m, k, :], wk[rows, m, :], wk[rows, m + 2, :],
                                            ALU.add).then_inc(s_setup, 1)
            dve.wait_ge(s_setup, 9)
            for k in range(2):
                rows = slice(k * C, (k + 1) * C)
                nc.vector.tensor_tensor(wbd[rows, 0, k, :], wk[rows, 0, :], wbd[rows, 2, k, :],
                                        ALU.subtract).then_inc(s_wbd, 1)
            dve.wait_ge(s_mhi, 1)
            nc.vector.tensor_tensor(m_table[C:P], bank[C:P, 2:4, :].rearrange("p a (h n) -> p (a h) n", n=P),
                                    m_table[C:P].bitcast(F32), ALU.subtract).then_inc(s_mlo, 1)
            for t in range(NT):
                dve.wait_ge(s_u, t + 1)
                src = bank[:, 4 * (t % 2):4 * (t % 2) + 4, 0:6 * C].rearrange("p b (k n) -> p b k n", k=3)
                dst = x0[:, t].rearrange("p (b n) -> p b n", b=NP)
                nc.vector.tensor_tensor(dst, src[:, :, 0], dst, ALU.add).then_inc(s_ud, 1)
            for t in range(NT):
                dve.wait_ge(s_adj[t], 16)
                nc.vector.tensor_tensor(dscr[:, t, :], graph[:, t, t * P:(t + 1) * P], ident[:],
                                        ALU.mult).then_inc(s_bad, 1)
            dve.wait_ge(s_bad, NT)
            nc.vector.reduce_sum(diag[:], dscr, AX_X).then_inc(s_bad, 1)
            for t in range(NT):
                nc.vector.tensor_reduce(lows[:, t:t + 1], graph[:, t, :], AX_X, ALU.min).then_inc(s_bad, 1)
            dve.wait_ge(s_bad, 2 * NT + 1)
            nc.vector.tensor_reduce(bad[:, 0:1], lows, AX_X, ALU.min).then_inc(s_bad, 1)
            nc.vector.tensor_reduce(bad[:, 1:2], diag[:], AX_X, ALU.min).then_inc(s_bad, 1)
            dve.wait_ge(s_bad, 2 * NT + 3)
            nc.vector.tensor_scalar(bad[:, 2:3], bad[:, 0:1], 0.0, None, ALU.is_lt).then_inc(s_bad, 1)
            dve.wait_ge(s_bad, 2 * NT + 4)
            nc.vector.scalar_tensor_tensor(out=bad[:, 3:4], in0=bad[:, 1:2], scalar=0.0, in1=bad[:, 2:3],
                                           op0=ALU.is_le, op1=ALU.max).then_inc(s_bad, 1)
            for t in range(1, NT, 2):
                dve.wait_ge(s_tr, t + 1)
                nc.vector.tensor_copy(graph_t[:, :, t * P:(t + 1) * P],
                                      bank[:, 2 * (t % 2):2 * (t % 2) + 2, :].rearrange("p a (j n) -> p (a j) n", n=P)
                                      ).then_inc(s_tc[1], 1)
            for t in range(NT):
                dve.wait_ge(s_av, t + 1)
                nc.vector.scalar_tensor_tensor(out=v[:, t], in0=bank[:, t % 2, :], scalar=2.0, in1=v[:, t],
                                               op0=ALU.mult, op1=ALU.add).then_inc(s_v, 1)
            dve.wait_ge(s_badt, 1)
            nc.vector.tensor_reduce(badrow[:], bank[0:1, 2, 0:P], AX_X, ALU.max).then_inc(s_bad, 1)
            dve.wait_ge(s_bad, 2 * NT + 6)
            nc.vector.tensor_copy(general[0:1, :], badrow[:]).then_inc(s_bad, 1)

            def low_part(t):
                dve.wait_ge(s_hi, t + 1)
                nc.vector.tensor_tensor(x_lo[:, :, t * P:(t + 1) * P],
                                        bank[:, 4 + 2 * (t % 2):6 + 2 * (t % 2), :].rearrange("p a (b n) -> p (a b) n", n=P),
                                        x_hi[:, :, t * P:(t + 1) * P].bitcast(F32), ALU.subtract).then_inc(s_lo, 1)

            for t in range(NT):
                k = t % 2
                dve.wait_ge(s_av, NT + t + 1)
                if t == 0:
                    dve.wait_ge(s_own, NT)
                nc.vector.tensor_tensor(resid[:, k].rearrange("p b c -> p (b c)"), bank[:, t % 2, :], x0[:, t],
                                        ALU.add).then_inc(s_r, 1)
                dve.wait_ge(s_r, 4 * t + 1)
                nc.vector.reduce_sum(stat[:, k, 0], resid[:, k], AX_X).then_inc(s_ln, 1)
                if t >= 1:
                    low_part(t - 1)
                dve.wait_ge(s_lp, 3 * t + 1)
                nc.vector.tensor_tensor(cen[:, k], resid[:, k],
                                        stat[:, k, 1].rearrange("p (b c) -> p b c", c=1).broadcast_to([P, B, C]),
                                        ALU.add).then_inc(s_r, 1)
                dve.wait_ge(s_r, 4 * t + 2)
                nc.vector.tensor_tensor(sq[:, k], cen[:, k], cen[:, k], ALU.mult).then_inc(s_r, 1)
                dve.wait_ge(s_r, 4 * t + 3)
                nc.vector.reduce_sum(stat[:, k, 2], sq[:, k], AX_X).then_inc(s_ln, 1)
                dve.wait_ge(s_lp, 3 * t + 3)
                if t >= 2:
                    dve.wait_ge(s_st[t % 2], 16 * (t // 2))
                    dve.wait_ge(s_t1, t - 1)
                nc.vector.tensor_tensor(x1[:, k], cen[:, k].rearrange("p b (k c) -> p b k c", k=1).broadcast_to([P, B, 2, C]),
                                        stat[:, k, 3].rearrange("p (b k c) -> p b k c", c=1, k=1).broadcast_to([P, B, 2, C]),
                                        ALU.mult).then_inc(s_x1, 1)
                dve.wait_ge(s_x1, t + 1)
                nc.vector.memset(bad[:, 0:1], 0.0).then_inc(s_r, 1)
            low_part(NT - 1)

        @block.tensor
        def _(pe):
            pe.wait_ge(s_id, 1)
            pe.wait_ge(s_w, 96)
            for h in range(H):
                last = nc.tensor.transpose(bank[:, 0, h * C:(h + 1) * C], w_rows[:, h, :], ident[0:C, 0:C])
            nc.tensor.transpose(bank[:, 1, 0:H], bias_rows[:], ident[0:H, 0:H]).then_inc(s_wtr, 1)
            pe.wait_ge(s_x, 16 * B)
            for g in range(NT // 2):
                if g >= 2:
                    pe.wait_ge(s_xtc, g - 1)
                for t in range(2 * g, 2 * g + 2):
                    for b in range(NP):
                        last = nc.tensor.transpose(bank[:, 4 + 2 * (g % 2) + t % 2, b * P:(b + 1) * P],
                                                   x0[:, t, b * P:(b + 1) * P], ident[:])
                last.then_inc(s_xtr, 1)
            pe.wait_ge(s_wtc, 2)
            for h in range(H):
                wt = w_t[:, h].rearrange("p k c -> p (k c)")
                last = nc.tensor.matmul(bank[:, 2 + h // 4, (h % 4) * P:(h % 4 + 1) * P], wt, wt, start=True, stop=True)
            last.then_inc(s_m, 1)
            pe.wait_ge(s_wbd, 2)
            pe.wait_ge(s_xtc, NT // 2)
            pe.wait_ge(s_mlo, 1)
            for t in range(NT):
                if t >= 2:
                    pe.wait_ge(s_uc, t - 1)
                    pe.wait_ge(s_ud, t - 1)
                for b in range(NP):
                    last = nc.tensor.matmul(bank[:, 4 * (t % 2) + b, 0:6 * C], xt[:, b, t * P:(t + 1) * P],
                                            wbd[:].rearrange("p k b c -> p (k b c)"), start=True, stop=True)
                last.then_inc(s_u, 1)
            pe.wait_ge(s_uc, NT)
            pe.wait_ge(s_ud, NT)
            for t in range(NT):
                pe.wait_ge(s_adj[t], 16)
                if t >= 2:
                    pe.wait_ge(s_tc[t % 2], t // 2)
                for j in range(NT):
                    last = nc.tensor.transpose(bank[:, 2 * (t % 2) + j // 4, (j % 4) * P:(j % 4 + 1) * P],
                                               graph[:, t, j * P:(j + 1) * P], ident[:])
                last.then_inc(s_tr, 1)
            for k in range(2):
                pe.wait_ge(s_tc[k], NT // 2)
            for t in range(NT):
                if t >= 2:
                    pe.wait_ge(s_v, t - 1)
                for j in range(NT):
                    last = nc.tensor.matmul(bank[:, t % 2, :], graph_t[:, j, t * P:(t + 1) * P], u2[:, j, :],
                                            start=(j == 0), stop=(j == NT - 1))
                last.then_inc(s_av, 1)
            pe.wait_ge(s_bad, 2 * NT + 5)
            nc.tensor.transpose(bank[0:1, 2, 0:P], bad[:, 3:4], ident[:]).then_inc(s_badt, 1)
            pe.wait_ge(s_v, NT)

            def turn_x1(t):
                pe.wait_ge(s_x1, t + 1)
                if t >= 2:
                    pe.wait_ge(s_lo, t - 1)
                for b in range(B):
                    src = x1[:, t % 2, b].rearrange("p k c -> p (k c)")
                    last = nc.tensor.transpose(bank[:, 4 + 2 * (t % 2) + b // 4, (b % 4) * P:(b % 4 + 1) * P],
                                               src, ident[:])
                last.then_inc(s_t1, 1)

            for t in range(NT):
                if t >= 2:
                    pe.wait_ge(s_r, 4 * (t - 2) + 1)
                for j in range(NT):
                    last = nc.tensor.matmul(bank[:, t % 2, :], graph_t[:, j, t * P:(t + 1) * P], v[:, j, :],
                                            start=(j == 0), stop=(j == NT - 1))
                last.then_inc(s_av, 1)
                if t >= 1:
                    turn_x1(t - 1)
            turn_x1(NT - 1)


def attention(nc, ctx, sem, env):
    wh, wout, out = (env[k] for k in ("wh", "wout", "out"))
    B, N, C, H, D, NT, HT, JOBS1, JOBS = (env[k] for k in ("B", "N", "C", "H", "D", "NT", "HT", "JOBS1", "JOBS"))
    graph, x_hi, x_lo, m_table, ident, dup, sel, head_bias, out_bias, general, x1_dram = (
        env[k] for k in ("graph", "x_hi", "x_lo", "m_table", "ident", "dup", "sel", "head_bias", "out_bias",
                         "general", "x1_dram"))

    def sb(name, shape, dt=F32):
        return ctx.enter_context(nc.sbuf_tensor(name, shape, dt))

    def ps(name, shape):
        return ctx.enter_context(nc.psum_tensor(name, shape, F32))

    scores = ps("scores", [P, 2, N])
    turned = ps("turned", [P, NT, P])
    mixed = ps("mixed", [P, BANK])
    small = ps("small", [P, BANK])

    gated = sb("gated", [P, 2, N])
    prob = sb("prob", [P, 4, N])
    prob_t = sb("prob_t", [P, 2, NT, BANK])
    y_parts = sb("y_parts", [P, 2, N], F32R)
    x_rows = sb("x_rows", [P, 2, NT * C])
    m_now = sb("m_now", [P, 2, P], F32R)
    bias_now = sb("bias_now", [P, 2, 2])
    w_now = sb("w_now", [P, 2, D])
    wout_now = sb("wout_now", [P, 2, C])
    recip_b = sb("recip_b", [P, 2, BANK])
    mixed_n = sb("mixed_n", [P, 2, BANK])
    head_neg = sb("head_neg", [P, 2, BANK])
    head_act = sb("head_act", [P, 2, BANK])
    h_acc = sb("h_acc", [P, B, BANK])
    y_raw = sb("y_raw", [P, BANK])
    row_max = sb("row_max", [P, NT])
    neg_max = sb("neg_max", [P, NT])
    mask_at = sb("mask_at", [P, NT])
    row_sum = sb("row_sum", [P, 2, NT])
    recip = sb("recip", [P, 2, NT])
    fin, fin2 = (head_neg[:, k].rearrange("p (t c) -> p t c", c=C) for k in range(2))
    x1_b, y_out = (head_act[:, k].rearrange("p (t c) -> p t c", c=C) for k in range(2))
    h_now = m_table[:, 0:BANK // P].rearrange("p h n -> p (h n)").bitcast(F32)
    stat = sb("fstat", [P, 4, NT])
    idle = sb("idle", [P, NT])
    consts = sb("consts", [P, 5, NT])

    s_scores = sem("scores_ready")
    s_gated = sem("gated_ready")
    s_shift = sem("shift_ready")
    s_exp = sem("exp_ready")
    s_prob = sem("prob_ready")
    s_turned = sem("turned_ready")
    s_prob_t = sem("prob_t_ready")
    s_mixed = sem("mixed_ready")
    s_recip = sem("recip_ready")
    s_rst = sem("recip_stored")
    s_rbc = [sem(f"recip_spread{a}") for a in range(2)]
    s_norm = sem("mixed_n_ready")
    s_post = sem("post_product_ready")
    s_raw = sem("head_split_ready")
    s_act = sem("head_act_ready")
    s_out1 = sem("wout_product_ready")
    s_acc = sem("h_acc_ready")
    s_zero = sem("h_acc_zeroed")
    s_y = sem("y_product_ready")
    s_yhi = sem("y_high_ready")
    s_ylo = sem("y_low_ready")
    s_hsp = sem("h_parts_spread")
    s_hrow = sem("h_rows_product_ready")
    s_hrc = sem("h_rows_ready")
    s_fin = sem("fin_ready")
    s_fd = sem("final_steps_dve")
    s_fs = sem("final_sums")
    s_fp = sem("final_steps_pool")
    s_m = [sem(f"m_loaded{k}") for k in range(2)]
    s_xr = [sem(f"x_rows_loaded{k}") for k in range(2)]
    s_wl = [sem(f"w_loaded{k}") for k in range(2)]
    s_x1 = sem("x1_b_loaded")
    s_store = sem("out_stored")
    s_consts = sem("consts_ready")
    s_gen = sem("general_dve")

    def kind(n):
        return 0 if n < 0 or n >= JOBS else 1 if n < JOBS1 else 2

    def run(eng, body):
        def one(n):
            body(Job(n // 2, n % 2), kind(n + 1), kind(n), kind(n - 1), kind(n - 2))

        for n in range(2):
            one(n)
        with eng.Fori(1, JOBS1 // 2 - 1) as pair:
            for odd in range(2):
                body(Job(pair, odd), 1, 1, 1, 1)
        for n in range(JOBS1 - 2, JOBS1 + 2):
            one(n)
        with eng.Fori(JOBS1 // 2 + 1, JOBS // 2 - 1) as pair:
            for odd in range(2):
                body(Job(pair, odd), 2, 2, 2, 2)
        for n in range(JOBS - 2, JOBS + 2):
            one(n)

    def batch(job, k):
        return job.pair // (H // 2) if k == 1 else (job.pair - JOBS1 // 2) * 2 + job.odd

    def head(job):
        return (job.pair % (H // 2)) * 2 + job.odd

    recip_dram = nc.dram_tensor("recip_scratch", [2, N], F32, kind="Internal").ap()
    block = ctx.enter_context(nc.Block())

    @block.sync
    def _(sp):
        def load_m(job):
            wait(sp, s_y, job.count(2, -2))
            sp.dma_start(m_now[:, job.odd].bitcast(F32), m_table[:, head(job)].bitcast(F32)).then_inc(s_m[job.odd], 16)

        def load_rows(job):
            wait(sp, s_mixed, job.count(2, -2))
            sp.dma_start(x_rows[:, job.odd], x1_dram[batch(job, 1)]).then_inc(s_xr[job.odd], 16)

        def load_weights(job):
            wait(sp, s_out1, job.count(1, -1))
            sp.dma_start(bias_now[:, job.odd], head_bias[:, head(job)]).then_inc(s_wl[job.odd], 16)
            for k in range(2):
                sp.dma_start(w_now[k * C:(k + 1) * C, job.odd], wh[head(job)]).then_inc(s_wl[job.odd], 16)
            sp.dma_start(wout_now[:, job.odd], wout.rearrange("(h d) c -> h d c", h=H)[head(job)]
                         ).then_inc(s_wl[job.odd], 16)

        def spread_recip(job, a):
            row = recip_dram[job.odd, a * BANK:(a + 1) * BANK]
            sp.wait_ge(s_recip, job.count(2, a + 1))
            with nc.allow_non_contiguous_dma(reason="512 numbers"):
                sp.dma_start(row.rearrange("(t p) -> p t", p=P), recip[:, job.odd, a * HT:(a + 1) * HT]
                             ).then_inc(s_rst, 16)
            sp.wait_ge(s_rst, job.count(32, 16 * a + 16))
            sp.dma_start(recip_b[:, a], row.rearrange("(k n) -> k n", k=1).broadcast_to([P, BANK])
                         ).then_inc(s_rbc[a], 16)

        def body(job, nxt, now, bef, bef2):
            if now == 1 and not (isinstance(job.pair, int) and job.pair == JOBS1 // 2 - 1):
                load_m(job.back(-2))
            if now == 1:
                load_rows(job)
            if bef:
                spread_recip(job.back(1), 1)
            if now == 1:
                load_weights(job)
            if now:
                spread_recip(job, 0)
            if bef2 == 2:
                j2 = job.back(2)
                b = batch(j2, 2)
                sp.wait_ge(s_fd, j2.count(5, 5 - 5 * JOBS1))
                sp.dma_start(out[b].rearrange("(t p) c -> p t c", p=P), y_out).then_inc(s_store, 16)
            if bef == 2:
                j1 = job.back(1)
                if isinstance(j1.pair, int) and j1.pair == JOBS1 // 2 and j1.odd == 0:
                    sp.wait_ge(s_out1, JOBS1)
                wait(sp, s_fd, j1.count(5, 0 - 5 * JOBS1))
                sp.dma_start(x1_b.rearrange("p t c -> p (t c)"), x1_dram[batch(j1, 2)]).then_inc(s_x1, 16)

        for n in range(2):
            load_m(Job(0, n))
        run(sp, body)
        sp.wait_ge(s_store, 16 * B)

    @block.tensor
    def _(pe):
        def y_product(job, k, a):
            cols = slice(a * BANK, (a + 1) * BANK)
            b = batch(job, k)
            if k == 1:
                if a == 0:
                    pe.wait_ge(s_m[job.odd], job.pair * 16 + 16)
                nc.tensor.matmul(small[:], m_now[:, job.odd], x_hi[:, b, cols], start=True, stop=False)
                nc.tensor.matmul(small[:], m_now[:, job.odd], x_lo[:, b, cols],
                                 start=False, stop=True).then_inc(s_y, 1)
            else:
                pe.wait_ge(s_acc, b * H + H)
                nc.tensor.matmul(small[:], sel[:, a], h_acc[:, b], start=True, stop=True).then_inc(s_y, 1)

        def post_product(job, k, a):
            pe.wait_ge(s_norm, job.count(2, a + 1))
            if k == 1:
                pe.wait_ge(s_wl[job.odd], job.pair * 64 + 64)
                nc.tensor.matmul(small[:], w_now[:, job.odd], mixed_n[:, a], start=True,
                                 stop=True).then_inc(s_post, 1)
            else:
                for i in range(HT):
                    last = nc.tensor.matmul(small[:, i * C:(i + 1) * C], mixed_n[:, a, i * P:(i + 1) * P],
                                            dup[:], start=True, stop=True)
                last.then_inc(s_post, 1)

        def post_free(job, k, a):
            if k == 1:
                wait(pe, s_raw, job.count(2, a + 1))
            elif k == 2:
                pe.wait_ge(s_fin, job.count(2, a + 1 - 2 * JOBS1))

        def body(job, nxt, now, bef, bef2):
            j1, j2, jn = job.back(1), job.back(2), job.back(-1)
            def mix(t):
                a, pair = t // HT, t % HT
                if pair == 0:
                    pe.wait_ge(s_prob_t, j1.count(NT, a * HT + HT))
                    wait(pe, s_norm, j1.count(2, a))
                if t == 0:
                    if bef == 1:
                        pe.wait_ge(s_xr[j1.odd], j1.pair * 16 + 16)
                    else:
                        pe.wait_ge(s_hrc, j1.count(1, 1 - JOBS1))
                for e in range(2):
                    m = 2 * pair + e
                    last = nc.tensor.matmul(mixed[e * C:(e + 1) * C, :], x_rows[:, j1.odd, m * C:(m + 1) * C],
                                            prob_t[:, a, m, :], start=(pair == 0), stop=(pair == HT - 1))
                if pair == HT - 1:
                    last.then_inc(s_mixed, 1)

            for t in range(NT):
                if bef and t % HT == HT - 1:
                    mix(t)
                if now:
                    wait(pe, s_gated, job.count(NT, t - 1))
                    if t == 0:
                        pe.wait_ge(s_ylo, job.count(2, 2))
                        if now == 2:
                            pe.wait_ge(s_hsp, job.count(4, 4 - 4 * JOBS1))
                    b = batch(job, now)
                    for a in range(2):
                        cols = slice(a * BANK, (a + 1) * BANK)
                        lhs = y_parts[:, job.odd, t * P:(t + 1) * P]
                        nc.tensor.matmul(scores[:, t % 2, cols], lhs, x_hi[:, b, cols], start=True, stop=False)
                        last = nc.tensor.matmul(scores[:, t % 2, cols], lhs, x_lo[:, b, cols], start=False, stop=True)
                    last.then_inc(s_scores, 1)
                if bef and 0 < t % HT < HT - 1:
                    mix(t)
                if (t >= 3 and now) or (t < 3 and bef):
                    pe.wait_ge(s_prob, job.count(NT, t - 2))
                    wait(pe, s_prob_t, job.count(NT, t - 3))
                    for m in range(NT):
                        last = nc.tensor.transpose(turned[:, m, :], prob[:, (t - 3) % 4, m * P:(m + 1) * P], ident[:])
                    last.then_inc(s_turned, 1)
                if t == 1 and bef2:
                    post_free(j2, bef2, 0)
                    post_product(j2, bef2, 1)
                if t == 3 and bef2 == 1:
                    pe.wait_ge(s_act, j2.count(2, 2))
                    for a in range(2):
                        last = nc.tensor.matmul(small[a * C:(a + 1) * C, :], wout_now[:, j2.odd], head_act[:, a],
                                                start=True, stop=True)
                    last.then_inc(s_out1, 1)
                if t == 3 and now == 2:
                    if bef2 == 1:
                        pe.wait_ge(s_acc, j2.count(1, 1))
                    else:
                        post_free(j2, bef2, 1)
                    for i in range(HT):
                        last = nc.tensor.transpose(small[:, i * P:(i + 1) * P], h_now[:, i * P:(i + 1) * P], ident[:])
                    last.then_inc(s_hrow, 1)
                if t in (5, 6) and nxt:
                    if t == 5 and bef2 == 1:
                        pe.wait_ge(s_acc, j2.count(1, 1))
                    if t == 5 and now == 2:
                        pe.wait_ge(s_hrc, job.count(1, 1 - JOBS1))
                    wait(pe, s_yhi, jn.count(2, t - 5))
                    y_product(jn, nxt, t - 5)
                if t == 7 and bef:
                    if nxt:
                        pe.wait_ge(s_yhi, jn.count(2, 2))
                    else:
                        post_free(j2, bef2, 1)
                        if now == 2:
                            pe.wait_ge(s_hrc, job.count(1, 1 - JOBS1))
                    post_product(j1, bef, 0)
                if bef and t % HT == 0:
                    mix(t)

        y_product(Job(0, 0), 1, 0)
        pe.wait_ge(s_yhi, 1)
        y_product(Job(0, 0), 1, 1)
        run(pe, body)

    @block.scalar
    def _(act):
        def y_high(job, k, a):
            cols = slice(a * BANK, (a + 1) * BANK)
            act.wait_ge(s_y, job.count(2, a + 1))
            if k == 2:
                wait(act, s_hrow, job.count(1, -JOBS1))
                rows = slice(a * C, (a + 1) * C)
                nc.scalar.activation(h_now[rows, :], small[rows, :], ACT.Copy)
            nc.scalar.activation(y_parts[:, job.odd, cols], small[:], ACT.Copy)
            wait(act, s_ylo, job.count(2, a))
            nc.scalar.activation(y_raw[:], small[:], ACT.Copy).then_inc(s_yhi, 1)

        def head_out(job, a):
            act.wait_ge(s_post, job.count(2, a + 1))
            wait(act, s_out1, job.count(1, 0))
            nc.scalar.activation(head_act[:, a], small[:], ACT.Relu, bias=bias_now[:, job.odd, 0:1], scale=1.0)
            nc.scalar.activation(head_neg[:, a], small[:], ACT.Relu, bias=bias_now[:, job.odd, 1:2],
                                 scale=-SLOPE).then_inc(s_raw, 1)

        def body(job, nxt, now, bef, bef2):
            j1, j2, jn = job.back(1), job.back(2), job.back(-1)
            for t in range(NT):
                if (t >= 1 and now) or (t < 1 and bef):
                    act.wait_ge(s_shift, job.count(NT, t))
                    wait(act, s_turned, job.count(NT, t - 4))
                    k = (t - 1) % NT
                    nc.scalar.activation(prob[:, k % 4], gated[:, k % 2], ACT.Exp, bias=neg_max[:, k:k + 1],
                                         scale=1.0).then_inc(s_exp, 1)
                if (t >= 3 and now) or (t < 3 and bef):
                    k = (t - 3) % NT
                    act.wait_ge(s_turned, job.count(NT, t - 2))
                    if k % HT == 0:
                        wait(act, s_mixed, (job if t >= 3 else j1).count(2, k // HT - 1))
                    nc.scalar.activation(prob_t[:, k // HT, :, (k % HT) * P:(k % HT + 1) * P], turned[:],
                                         ACT.Copy).then_inc(s_prob_t, 1)
                if t == 1 and bef2 == 1:
                    head_out(j2, 1)
                if t == 3 and now == 2:
                    act.wait_ge(s_hrow, job.count(1, 1 - JOBS1))
                    act.wait_ge(s_mixed, job.count(2, -2))
                    nc.scalar.activation(x_rows[:, job.odd].rearrange("p (a i c) -> p i a c", a=2, c=C),
                                         small[:].rearrange("p (i a c) -> p i a c", a=2, c=C),
                                         ACT.Copy).then_inc(s_hrc, 1)
                if t in (5, 6) and nxt:
                    y_high(jn, nxt, t - 5)
                if t == 7 and bef == 1:
                    head_out(j1, 0)

        for a in range(2):
            y_high(Job(0, 0), 1, a)
        run(act, body)

    @block.gpsimd
    def _(pool):
        for k, value in enumerate((-1.0, -0.5, -1.0 / C, 1.0 / C, EPS)):
            nc.gpsimd.memset(consts[:, k], value).then_inc(s_consts, 1)
        pool.wait_ge(s_consts, 5)

        def y_low(job, k, a, shifts):
            cols = slice(a * BANK, (a + 1) * BANK)
            pool.wait_ge(s_yhi, job.count(2, a + 1))
            wait(pool, s_shift, shifts)
            if k == 2:
                pool.wait_ge(s_hsp, job.count(4, 2 * a + 2 - 4 * JOBS1))
            nc.gpsimd.tensor_tensor(y_parts[C:P, job.odd, cols], y_raw[C:P, :],
                                    y_parts[C:P, job.odd, cols].bitcast(F32), ALU.subtract).then_inc(s_ylo, 1)
            pool.wait_ge(s_ylo, job.count(2, a + 1))

        def leaky(job, a):
            pool.wait_ge(s_raw, job.count(2, a + 1))
            nc.gpsimd.tensor_tensor(head_act[:, a], head_act[:, a], head_neg[:, a], ALU.subtract).then_inc(s_act, 1)

        def body(job, nxt, now, bef, bef2):
            j1, j2, jn = job.back(1), job.back(2), job.back(-1)
            for t in range(NT):
                if now:
                    pool.wait_ge(s_gated, job.count(NT, t + 1))
                    nc.gpsimd.tensor_tensor(neg_max[:, t:t + 1], row_max[:, t:t + 1], consts[:, 0, 0:1], ALU.mult)
                    nc.gpsimd.tensor_scalar(mask_at[:, t:t + 1], row_max[:, t:t + 1], 0.0, NEVER, ALU.is_le,
                                            ALU.mult).then_inc(s_shift, 1)
                if t == 2 and bef2 == 1:
                    leaky(j2, 1)
                if t in (5, 6) and nxt:
                    y_low(jn, nxt, t - 5, job.count(NT, t + 1))
                if t == 7 and bef == 1:
                    leaky(j1, 0)
                if bef2 == 2 and t == 3:
                    pool.wait_ge(s_fs, j2.count(2, 1 - 2 * JOBS1))
                    nc.gpsimd.tensor_tensor(stat[:, 1], stat[:, 0], consts[:, 2], ALU.mult).then_inc(s_fp, 1)
                if bef2 == 2 and t == 4:
                    pool.wait_ge(s_fs, j2.count(2, 2 - 2 * JOBS1))
                    nc.gpsimd.tensor_tensor(stat[:, 3], stat[:, 2], consts[:, 3], ALU.mult).then_inc(s_fp, 1)
                    pool.wait_ge(s_fp, j2.count(4, 2 - 4 * JOBS1))
                    nc.gpsimd.tensor_tensor(stat[:, 3], stat[:, 3], consts[:, 4], ALU.add).then_inc(s_fp, 1)
                    pool.wait_ge(s_fp, j2.count(4, 3 - 4 * JOBS1))
                    nc.gpsimd.tensor_tensor(stat[:, 3], stat[:, 3], consts[:, 1], ALU.pow).then_inc(s_fp, 1)

        for a in range(2):
            y_low(Job(0, 0), 1, a, 0)
        run(pool, body)

    @block.vector
    def _(dve):
        def h_parts(job, a):
            cols = slice(a * BANK, (a + 1) * BANK)
            dve.wait_ge(s_yhi, job.count(2, a + 1))
            nc.vector.tensor_scalar(x_hi[:, batch(job, 2), cols], y_parts[:, job.odd, cols].bitcast(F32), 1.0, None,
                                    ALU.mult).then_inc(s_hsp, 1)
            nc.vector.tensor_tensor(x_lo[:, batch(job, 2), cols], y_raw[:],
                                    y_parts[:, job.odd, cols].bitcast(F32), ALU.subtract).then_inc(s_hsp, 1)

        def reciprocals(job, a):
            dve.wait_ge(s_prob, job.count(NT, a * HT + HT))
            cols = slice(a * HT, (a + 1) * HT)
            nc.vector.reciprocal(recip[:, job.odd, cols], row_sum[:, job.odd, cols]).then_inc(s_recip, 1)

        def normalise(job, a):
            dve.wait_ge(s_mixed, job.count(2, a + 1))
            dve.wait_ge(s_rbc[a], job.count(16, 16))
            wait(dve, s_post, job.count(2, a - 1))
            nc.vector.tensor_tensor(mixed_n[:, a], mixed[:], recip_b[:, a], ALU.mult).then_inc(s_norm, 1)

        def accumulate(job):
            dve.wait_ge(s_out1, job.count(1, 1))
            wait(dve, s_acc, job.count(1, 0))
            b = batch(job, 1)
            nc.vector.tensor_tensor(h_acc[:, b], small[:], h_acc[:, b], ALU.add).then_inc(s_acc, 1)

        def final_rows(job, a):
            dve.wait_ge(s_post, job.count(2, a + 1))
            if isinstance(job.pair, int):
                wait(dve, s_fd, job.count(5, 1 - 5 * JOBS1 - 5))
            else:
                dve.wait_ge(s_gated, job.count(NT, 2 * NT))
            nc.vector.tensor_tensor(fin[:, a * HT:(a + 1) * HT, :],
                                    small[:, 0:HT * C].rearrange("p (t c) -> p t c", c=C),
                                    out_bias[:].rearrange("p (a c) -> p a c", a=1).broadcast_to([P, HT, C]),
                                    ALU.add).then_inc(s_fin, 1)

        def spread(row):
            return row.rearrange("p (t c) -> p t c", c=1).broadcast_to([P, NT, C])

        def final_steps(job, part):
            n = job.count(1, -JOBS1)
            if part == 0:
                dve.wait_ge(s_fin, n * 2 + 2)
                wait(dve, s_fd, n * 5)
                nc.vector.scalar_tensor_tensor(out=fin2, in0=fin, scalar=SLOPE, in1=fin, op0=ALU.mult,
                                               op1=ALU.max).then_inc(s_fd, 1)
                dve.wait_ge(s_fd, n * 5 + 1)
                dve.wait_ge(s_x1, n * 16 + 16)
                nc.vector.tensor_tensor(fin2, fin2, x1_b, ALU.add).then_inc(s_fd, 1)
                dve.wait_ge(s_fd, n * 5 + 2)
                nc.vector.reduce_sum(stat[:, 0], fin2, AX_X).then_inc(s_fs, 1)
            elif part == 1:
                dve.wait_ge(s_fp, n * 4 + 1)
                dve.wait_ge(s_fs, n * 2 + 1)
                nc.vector.tensor_tensor(fin2, fin2, spread(stat[:, 1]), ALU.add).then_inc(s_fd, 1)
                dve.wait_ge(s_fd, n * 5 + 3)
                wait(dve, s_store, n * 16)
                nc.vector.tensor_tensor(y_out, fin2, fin2, ALU.mult).then_inc(s_fd, 1)
                dve.wait_ge(s_fd, n * 5 + 4)
                nc.vector.reduce_sum(stat[:, 2], y_out, AX_X).then_inc(s_fs, 1)
            else:
                dve.wait_ge(s_fp, n * 4 + 4)
                dve.wait_ge(s_fs, n * 2 + 2)
                nc.vector.tensor_tensor(y_out, fin2, spread(stat[:, 3]), ALU.mult).then_inc(s_fd, 1)

        def pipeline(general_graph):
            def body(job, nxt, now, bef, bef2):
                j1, j2, jn = job.back(1), job.back(2), job.back(-1)
                for t in range(NT):
                    if t == 2 and bef:
                        reciprocals(j1, 1)
                    if t == 6 and now:
                        reciprocals(job, 0)
                    if (t >= 2 and now) or (t < 2 and bef):
                        k = (t - 2) % NT
                        dve.wait_ge(s_exp, job.count(NT, t - 1))
                        nc.vector.scalar_tensor_tensor(
                            out=prob[:, k % 4], in0=gated[:, k % 2], scalar=mask_at[:, k:k + 1], in1=prob[:, k % 4],
                            op0=ALU.not_equal, op1=ALU.mult,
                            accum_out=row_sum[:, (job if t >= 2 else j1).odd, k:k + 1]).then_inc(s_prob, 1)
                    if t == 0 and bef2:
                        normalise(j2, 1)
                    if t == 0 and bef2 == 2:
                        final_rows(j2, 0)
                    if t == 2 and bef2 == 2:
                        final_rows(j2, 1)
                    if t == 3 and bef2 == 2:
                        final_steps(j2, 0)
                    if t == (4 if now == 2 else 5) and bef2 == 1:
                        accumulate(j2)
                    if t == 4 and bef:
                        normalise(j1, 0)
                    if t == 4 and bef2 == 2:
                        final_steps(j2, 1)
                    if t in (6, 7) and nxt == 2:
                        h_parts(jn, t - 6)
                    if t == 6 and bef2 == 2:
                        final_steps(j2, 2)
                    if now:
                        n = job.count(2 * NT, 2 * t)
                        dve.wait_ge(s_scores, job.count(NT, t + 1))
                        wait(dve, s_prob, job.count(NT, t - 1))
                        nc.vector.memset(idle[:, t:t + 1], 0.0)
                        ins = nc.vector.tensor_tensor_reduce(
                            out=gated[:, t % 2], in0=scores[:, t % 2], in1=graph[:, t], scale=1.0, scalar=LOWEST,
                            op0=ALU.mult, op1=ALU.max, accum_out=row_max[:, t:t + 1])
                        if not general_graph:
                            ins.then_inc(s_gated, 1)
                        else:
                            ins.then_inc(s_gen, 1)
                            dve.wait_ge(s_gen, n + 1)
                            zeros = prob[:, t % 4]
                            nc.vector.tensor_scalar(zeros, gated[:, t % 2], 0.0, NEG_INF, ALU.is_equal,
                                                    ALU.mult).then_inc(s_gen, 1)
                            dve.wait_ge(s_gen, n + 2)
                            nc.vector.memset(idle[:, t:t + 1], 0.0)
                            nc.vector.tensor_tensor_reduce(
                                out=gated[:, t % 2], in0=gated[:, t % 2], in1=zeros, scale=1.0, scalar=LOWEST,
                                op0=ALU.add, op1=ALU.max, accum_out=row_max[:, t:t + 1]).then_inc(s_gated, 1)

            run(dve, body)

        nc.vector.memset(h_acc[:], 0.0).then_inc(s_zero, 1)
        dve.wait_ge(s_zero, 1)
        flag = dve.value_load(general[0:1, 0:1], min_val=0, max_val=1)
        with dve.If(flag == 0):
            pipeline(False)
        with dve.Else():
            pipeline(True)


_INS = ['x', 'adj', 'L0_gnn_weight', 'L0_gnn_bias', 'L1_gnn_Wh', 'L1_gnn_bh', 'L1_gnn_W_out', 'L1_gnn_b_out']


def kernel(**inputs):
    import numpy as _np
    import concourse.bacc as _bacc
    from concourse import mybir as _mybir
    from concourse.bass_utils import run_bass_kernel_spmd as _run

    nc = _bacc.Bacc("TRN2", target_bir_lowering=False, num_devices=1)
    arrays, args = {}, []
    for name in _INS:
        a = _np.ascontiguousarray(inputs[name])
        arrays[f"in_{name}"] = a
        args.append(nc.dram_tensor(f"in_{name}", a.shape, _mybir.dt.from_np(a.dtype), kind="ExternalInput").ap())
    args.append(nc.dram_tensor("out_0", inputs['x'].shape, _mybir.dt.float32, kind="ExternalOutput").ap())
    program(nc, *args)
    r = _run(nc, [arrays], core_ids=[0])
    return r.results[0]["out_0"]
```

```python
from contextlib import ExitStack

import concourse.bass as bass
from concourse import mybir

P = 128
ALU = mybir.AluOpType
ACT = mybir.ActivationFunctionType
F32 = mybir.dt.float32
F32R = mybir.dt.float32r
I32 = mybir.dt.int32
AX_X = mybir.AxisListType.X

NEG_INF = -1e16
NEVER = 1e30
LOWEST = -3e38
SLOPE = 0.01
EPS = 1e-5
BANK = 512


class Job:

    def __init__(self, pair, odd, shift=0):
        n = odd + shift
        self.pair = pair + n // 2
        self.odd = n % 2
        self.at = (pair, odd)

    def back(self, n):
        return Job(self.at[0], self.at[1], -n)

    def count(self, each, plus=0):
        return self.pair * (2 * each) + (self.odd * each + plus)


def wait(eng, sem, value):
    if isinstance(value, int) and value <= 0:
        return
    eng.wait_ge(sem, value)


def program(nc, x, adj, w0, b0, wh, bh, wout, bout, out):
    B, N, C = x.shape
    H, _, D = wh.shape
    NT = N // P
    HT = NT // 2
    JOBS1 = B * H
    JOBS = JOBS1 + B
    assert 2 * C == P and D == P and N == 2 * BANK and H % 2 == 0 and B % 2 == 0

    with ExitStack() as ctx:
        def sb(name, shape, dt=F32, to=ctx):
            return to.enter_context(nc.sbuf_tensor(name, shape, dt))

        def sem(name):
            return ctx.enter_context(nc.semaphore(name))

        w_dram = nc.dram_tensor("w_scratch", [H, C, 2, D], F32, kind="Internal").ap()
        x1_dram = nc.dram_tensor("x1_scratch", [B, P, NT * C], F32, kind="Internal").ap()

        graph = sb("graph", [P, NT, N])
        x_hi = sb("x_hi", [P, B, N], F32R)
        x_lo = sb("x_lo", [P, B, N], F32R)
        m_table = sb("m_table", [P, H // 2, 2, C], F32R)
        m_now = sb("m_now", [P, P], F32R)
        ident = sb("ident", [P, P])
        dup = sb("dup", [P, C])
        sel = sb("sel", [P, 2, P])
        head_bias = sb("head_bias", [P, H, 2])
        out_bias = sb("out_bias", [P, C])
        general = sb("general", [P, 1], I32)

        prologue(nc, ctx, sem, locals())
        attention(nc, ctx, sem, locals())


def prologue(nc, ctx, sem, env):
    x, adj, w0, b0, wh, bh, bout = (env[k] for k in ("x", "adj", "w0", "b0", "wh", "bh", "bout"))
    B, N, C, H, NT = (env[k] for k in ("B", "N", "C", "H", "NT"))
    graph, x_hi, x_lo, m_table, m_now, ident, dup, sel, head_bias, out_bias, general, x1_dram, w_dram = (
        env[k] for k in ("graph", "x_hi", "x_lo", "m_table", "m_now", "ident", "dup", "sel", "head_bias",
                         "out_bias", "general", "x1_dram", "w_dram"))
    BC = B * C
    NP = B // 2
    assert B == NT and B == H
    with ExitStack() as tmp:
        def sb(name, shape, dt=F32):
            return tmp.enter_context(nc.sbuf_tensor(name, shape, dt))

        bank = tmp.enter_context(nc.psum_tensor("pro_psum", [P, 8, BANK], F32))
        x0 = sb("x0", [P, NT, BC])
        adj_hi = sb("adj_hi", [P, NT, N], F32R)
        adj_lo = x_lo
        u_hi, u_lo = (x_hi[:, k * NP:(k + 1) * NP].rearrange("p b n -> p (b n)").rearrange("p (t c) -> p t c", c=BC)
                      for k in range(2))
        v_hi = sb("v_hi", [P, NT, BC], F32R)
        v_lo = sb("v_lo", [P, NT, BC], F32R)
        wk = sb("wk", [P, 5, C])
        wbd = sb("wbd", [P, 3, 2, C])
        bias0 = sb("bias0", [P, C])
        rows = sb("rows", [P, 5, 2 * BC])
        resid, cen, sq = (rows[:, k].rearrange("p (k b c) -> p k b c", k=2, c=C) for k in range(3))
        x1 = rows[:, 3:5].rearrange("p k (b r c) -> p k b r c", r=2, c=C)
        stat = sb("stat", [P, 2, 4, B])
        half = sb("half", [P, B])
        diag = sb("diag", [P, NT])
        lows = sb("lows", [P, NT])
        xt = rows[:, 0:4].rearrange("p b n -> p (b n)").rearrange("p (b n) -> p b n", n=N)
        w_rows = x1[0:C, 1].rearrange("p b k c -> p b (k c)")
        w_hi, w_lo = (part[0:C, NT - 2:].rearrange("p t c -> p (t c)").rearrange("p (h d) -> p h d", h=H)
                      for part in (v_hi, v_lo))
        w_t = x1[:, 0]
        diag_tiles = rows[:, 2].rearrange("p (t n) -> p t n", n=P)
        bad = sb("bad", [P, 4])
        bias_rows = sb("bias_rows", [H, P])
        badrow = sb("badrow", [1, 1])

        s_blank = sem("p_blank")
        s_adj = [sem(f"p_adj{t}") for t in range(NT)]
        s_x = [sem(f"p_x_pair{b}") for b in range(NP)]
        s_wk = sem("p_w0")
        s_w = sem("p_weights")
        s_id = sem("p_ident")
        s_tr = sem("p_adj_turned")
        s_ahi = sem("p_adj_high")
        s_alo = sem("p_adj_low")
        s_xtr = sem("p_x_turned")
        s_xtc = sem("p_x_turned_copied")
        s_wbd = sem("p_w_combined")
        s_u = sem("p_u")
        s_uc = sem("p_u_high")
        s_ud = sem("p_u_low_and_own_part")
        s_own = sem("p_own_part")
        s_av = sem("p_adj_product")
        s_vhi = sem("p_v_high")
        s_vlo = sem("p_v_low")
        s_r = sem("p_resid")
        s_cen = sem("p_centred")
        s_sq = sem("p_squares")
        s_sum = sem("p_norm_sum")
        s_ssq = sem("p_norm_sum_of_squares")
        s_lp = sem("p_norm_pool")
        s_x1 = sem("p_x1")
        s_t1 = sem("p_x1_turned")
        s_hi = sem("p_x1_high")
        s_lo = sem("p_x1_low")
        s_st = [sem(f"p_x1_stored{k}") for k in range(2)]
        s_wtr = sem("p_w_turned")
        s_wtc = sem("p_w_turned_copied")
        s_m = sem("p_m")
        s_mhi = sem("p_m_high")
        s_mlo = sem("p_m_low")
        s_mfirst = sem("p_m_first")
        s_whi = sem("p_w_high")
        s_wlo = sem("p_w_low")
        s_wst = sem("p_w_parts_stored")
        s_bad = sem("p_bad")
        s_badt = sem("p_bad_turned")

        block = tmp.enter_context(nc.Block())

        def adj_banks(t):
            return bank[:, 2 * (t % 2):2 * (t % 2) + 2, :].rearrange("p a (j n) -> p (a j) n", n=P)

        def x1_banks(t):
            return bank[:, 4 + 2 * (t % 2):6 + 2 * (t % 2), :].rearrange("p a (b n) -> p (a b) n", n=P)

        def u_banks(t):
            return bank[:, 4 * (t % 2):4 * (t % 2) + 4, 0:4 * C].rearrange("p b (k n) -> p b k n", k=2)

        m_bank = bank[:, 6, :].rearrange("p (h k c) -> p h k c", k=2, c=C)

        @block.sync
        def _(sp):
            for t in range(NT):
                sp.dma_start(graph[:, t, :], adj[t * P:(t + 1) * P, :]).then_inc(s_adj[t], 16)
            sp.wait_ge(s_wlo, 1)
            for k, part in enumerate((w_hi, w_lo)):
                sp.dma_start(w_dram[:, :, k, :].rearrange("h c d -> c h d"), part.bitcast(F32)).then_inc(s_wst, 16)
            sp.wait_ge(s_wst, 32)
            for t in range(NT):
                sp.wait_ge(s_x1, t + 1)
                sp.dma_start(x1_dram.rearrange("b p (t c) -> p t b c", c=C)[:, t], x1[:, t % 2, :, 0]
                             ).then_inc(s_st[t % 2], 16)
            sp.wait_ge(s_mlo, 1)
            sp.dma_start(m_now[:].bitcast(F32), m_table[:, 0].bitcast(F32).rearrange("p k c -> p (k c)")
                         ).then_inc(s_mfirst, 16)
            for k in range(2):
                sp.wait_ge(s_st[k], 16 * (NT // 2))
            sp.wait_ge(s_mfirst, 16)

        @block.scalar
        def _(act):
            for k in range(2):
                act.dma_start(wk[k * C:(k + 1) * C], w0.rearrange("(k c) o -> c k o", c=C)).then_inc(s_wk, 16)
            for b in range(B):
                act.dma_start(x0[:, :, b * C:(b + 1) * C],
                              x[b].rearrange("(t p) c -> p t c", p=P)).then_inc(s_x[b // 2], 16)
            act.dma_start(bias0[:], b0.rearrange("(a c) -> a c", a=1).broadcast_to([P, C])).then_inc(s_w, 16)
            act.dma_start(out_bias[:], bout.rearrange("(a c) -> a c", a=1).broadcast_to([P, C])).then_inc(s_w, 16)
            act.dma_start(w_rows, wh.rearrange("h c d -> c h d")).then_inc(s_w, 16)
            act.dma_start(bias_rows[:], bh).then_inc(s_w, 16)
            for b in range(NP):
                for t in range(2 * b, 2 * b + 2):
                    act.wait_ge(s_tr, t + 1)
                    nc.scalar.activation(adj_hi[:, :, t * P:(t + 1) * P], adj_banks(t), ACT.Copy).then_inc(s_ahi, 1)
                act.wait_ge(s_xtr, b + 1)
                nc.scalar.activation(xt[:, b].rearrange("p (t n) -> p t n", n=P), x1_banks(b), ACT.Copy
                                     ).then_inc(s_xtc, 1)
            for t in range(NT):
                act.wait_ge(s_u, t + 1)
                nc.scalar.activation(u_hi[:, t].rearrange("p (b n) -> p b n", b=NP), u_banks(t)[:, :, 1],
                                     ACT.Copy).then_inc(s_uc, 1)
            act.wait_ge(s_w, 64)
            nc.scalar.activation(w_hi, w_rows, ACT.Copy).then_inc(s_whi, 1)
            for t in range(NT):
                act.wait_ge(s_av, t + 1)
                if t == NT - 2:
                    act.wait_ge(s_wst, 32)
                nc.scalar.activation(v_hi[:, t], bank[:, t % 2, :], ACT.Copy).then_inc(s_vhi, 1)
            act.wait_ge(s_wtr, 1)
            for k in range(2):
                nc.scalar.activation(w_t[:, :, k, :], bank[:, 4, :].rearrange("p (h c) -> p h c", h=H),
                                     ACT.Copy).then_inc(s_wtc, 1)
            for k, factor in enumerate((1.0, -SLOPE)):
                nc.scalar.activation(head_bias[:, :, k], bank[:, 5, 0:H], ACT.Copy, scale=factor)
            act.wait_ge(s_m, 1)
            nc.scalar.activation(m_table[:], m_bank, ACT.Copy).then_inc(s_mhi, 1)

            def high_part(t):
                act.wait_ge(s_t1, t + 1)
                nc.scalar.activation(x_hi[:, :, t * P:(t + 1) * P], x1_banks(t), ACT.Copy).then_inc(s_hi, 1)

            for t in range(NT):
                if t >= 2:
                    high_part(t - 2)
                act.wait_ge(s_cen, t + 1)
                nc.scalar.activation(sq[:, t % 2], cen[:, t % 2], ACT.Square).then_inc(s_sq, 1)
            high_part(NT - 2)
            high_part(NT - 1)

        @block.gpsimd
        def _(pool):
            nc.gpsimd.memset(ident[:], 0.0)
            nc.gpsimd.memset(wbd[:], 0.0)
            nc.gpsimd.memset(sel[:], 0.0)
            nc.gpsimd.memset(half[:], -0.5).then_inc(s_blank, 1)
            pool.wait_ge(s_blank, 1)
            nc.gpsimd.affine_select(out=ident[:], in_=ident[:], compare_op=ALU.not_equal, fill=1.0, base=0,
                                    pattern=[[-1, P]], channel_multiplier=1).then_inc(s_id, 1)
            pool.wait_ge(s_w, 64)
            for t in range(NT):
                pool.wait_ge(s_ud, t + 1)
                nc.gpsimd.tensor_tensor(x0[:, t].rearrange("p (b c) -> p b c", b=B),
                                        x0[:, t].rearrange("p (b c) -> p b c", b=B),
                                        bias0[:].rearrange("p (a c) -> p a c", a=1).broadcast_to([P, B, C]),
                                        ALU.add).then_inc(s_own, 1)
            for t in range(NT):
                pool.wait_ge(s_sum, t + 1)
                nc.gpsimd.tensor_scalar(stat[:, t % 2, 1], stat[:, t % 2, 0], -1.0 / C, 0.0,
                                        ALU.mult, ALU.add).then_inc(s_lp, 1)
                pool.wait_ge(s_ssq, t + 1)
                nc.gpsimd.tensor_scalar(stat[:, t % 2, 3], stat[:, t % 2, 2], 1.0 / C, EPS,
                                        ALU.mult, ALU.add).then_inc(s_lp, 1)
                pool.wait_ge(s_lp, 3 * t + 2)
                nc.gpsimd.tensor_tensor(stat[:, t % 2, 3], stat[:, t % 2, 3], half[:], ALU.pow).then_inc(s_lp, 1)

        @block.vector
        def _(dve):
            dve.wait_ge(s_id, 1)
            nc.vector.tensor_tensor(dup[:], ident[:, 0:C], ident[:, C:P], ALU.add)
            dve.wait_ge(s_blank, 1)
            for k in range(2):
                part = slice(k * C, (k + 1) * C)
                for i in range(2):
                    nc.vector.tensor_tensor(sel[part, k, i * C:(i + 1) * C], ident[part, 0:C], ident[part, C:P],
                                            ALU.add)
            dve.wait_ge(s_wk, 32)
            dve.wait_ge(s_blank, 1)
            diagonal = [slice(k * C, (k + 1) * C) for k in range(2)]
            for k, part in enumerate(diagonal):
                nc.vector.tensor_tensor(wbd[part, 2, k, :], wk[part, 1, :], wk[part, 3, :],
                                        ALU.add).then_inc(s_wbd, 1)
                nc.vector.tensor_tensor(wbd[part, 1, k, :], wk[part, 2, :], wk[part, 4, :],
                                        ALU.add).then_inc(s_wbd, 1)
            dve.wait_ge(s_wbd, 4)
            for k, part in enumerate(diagonal):
                nc.vector.tensor_tensor(wbd[part, 0, k, :], wk[part, 0, :], wbd[part, 1, k, :],
                                        ALU.subtract).then_inc(s_wbd, 1)
            dve.wait_ge(s_wbd, 6)
            for k, part in enumerate(diagonal):
                nc.vector.tensor_tensor(wbd[part, 1, k, :], wbd[part, 1, k, :], wbd[part, 1, k, :],
                                        ALU.add).then_inc(s_wbd, 1)
            for t in range(NT):
                dve.wait_ge(s_ahi, t + 1)
                nc.vector.tensor_tensor(adj_lo[:, :, t * P:(t + 1) * P], adj_banks(t),
                                        adj_hi[:, :, t * P:(t + 1) * P].bitcast(F32), ALU.subtract).then_inc(s_alo, 1)
            for t in range(NT):
                dve.wait_ge(s_uc, t + 1)
                dst = x0[:, t].rearrange("p (b n) -> p b n", b=NP)
                nc.vector.tensor_tensor(dst, u_banks(t)[:, :, 0], dst, ALU.add)
                nc.vector.tensor_tensor(u_lo[:, t].rearrange("p (b n) -> p b n", b=NP), u_banks(t)[:, :, 1],
                                        u_hi[:, t].bitcast(F32).rearrange("p (b n) -> p b n", b=NP),
                                        ALU.subtract).then_inc(s_ud, 1)
            dve.wait_ge(s_whi, 1)
            nc.vector.tensor_tensor(w_lo, w_rows, w_hi.bitcast(F32), ALU.subtract).then_inc(s_wlo, 1)
            for t in range(NT):
                nc.vector.tensor_reduce(lows[:, t:t + 1], graph[:, t, :], AX_X, ALU.min).then_inc(s_bad, 1)
                dve.wait_ge(s_vhi, t + 1)
                nc.vector.tensor_tensor(v_lo[:, t], bank[:, t % 2, :], v_hi[:, t].bitcast(F32),
                                        ALU.subtract).then_inc(s_vlo, 1)
            for t in range(NT):
                nc.vector.tensor_tensor(diag_tiles[:, t, :], graph[:, t, t * P:(t + 1) * P], ident[:],
                                        ALU.mult).then_inc(s_bad, 1)
            dve.wait_ge(s_bad, 2 * NT)
            nc.vector.reduce_sum(diag[:], diag_tiles, AX_X).then_inc(s_bad, 1)
            nc.vector.tensor_reduce(bad[:, 0:1], lows[:], AX_X, ALU.min).then_inc(s_bad, 1)
            dve.wait_ge(s_bad, 2 * NT + 2)
            nc.vector.tensor_reduce(bad[:, 1:2], diag[:], AX_X, ALU.min).then_inc(s_bad, 1)
            nc.vector.tensor_scalar(bad[:, 2:3], bad[:, 0:1], 0.0, None, ALU.is_lt).then_inc(s_bad, 1)
            dve.wait_ge(s_bad, 2 * NT + 4)
            nc.vector.scalar_tensor_tensor(out=bad[:, 3:4], in0=bad[:, 1:2], scalar=0.0, in1=bad[:, 2:3],
                                           op0=ALU.is_le, op1=ALU.max).then_inc(s_bad, 1)

            def residual(t):
                dve.wait_ge(s_av, NT + t + 1)
                if t == 0:
                    dve.wait_ge(s_own, NT)
                nc.vector.tensor_tensor(resid[:, t % 2].rearrange("p b c -> p (b c)"), bank[:, t % 2, :], x0[:, t],
                                        ALU.add).then_inc(s_r, 1)
                dve.wait_ge(s_r, t + 1)
                nc.vector.reduce_sum(stat[:, t % 2, 0], resid[:, t % 2], AX_X).then_inc(s_sum, 1)

            def low_part(t):
                dve.wait_ge(s_hi, t + 1)
                nc.vector.tensor_tensor(x_lo[:, :, t * P:(t + 1) * P], x1_banks(t),
                                        x_hi[:, :, t * P:(t + 1) * P].bitcast(F32), ALU.subtract).then_inc(s_lo, 1)

            residual(0)
            for t in range(NT):
                k = t % 2
                dve.wait_ge(s_lp, 3 * t + 1)
                if t >= 1:
                    dve.wait_ge(s_x1, t)
                nc.vector.tensor_tensor(cen[:, k], resid[:, k],
                                        stat[:, k, 1].rearrange("p (b c) -> p b c", c=1).broadcast_to([P, B, C]),
                                        ALU.add).then_inc(s_cen, 1)
                if t >= 2:
                    low_part(t - 2)
                if t == 0:
                    dve.wait_ge(s_mhi, 1)
                    nc.vector.tensor_tensor(m_table[C:P], m_bank[C:P], m_table[C:P].bitcast(F32),
                                            ALU.subtract).then_inc(s_mlo, 1)
                    dve.wait_ge(s_badt, 1)
                    nc.vector.tensor_reduce(badrow[:], bank[0:1, 2, 0:P], AX_X, ALU.max).then_inc(s_bad, 1)
                    dve.wait_ge(s_bad, 2 * NT + 6)
                    nc.vector.tensor_copy(general[0:1, :], badrow[:]).then_inc(s_bad, 1)
                dve.wait_ge(s_sq, t + 1)
                nc.vector.reduce_sum(stat[:, k, 2], sq[:, k], AX_X).then_inc(s_ssq, 1)
                if t + 1 < NT:
                    residual(t + 1)
                if t == NT - 1:
                    low_part(t - 1)
                dve.wait_ge(s_lp, 3 * t + 3)
                if t >= 2:
                    dve.wait_ge(s_st[k], 16 * (t // 2))
                    dve.wait_ge(s_t1, t - 1)
                twice = cen[:, k].rearrange("p b (k c) -> p b k c", k=1).broadcast_to([P, B, 2, C])
                factor = stat[:, k, 3].rearrange("p (b k c) -> p b k c", c=1, k=1).broadcast_to([P, B, 2, C])
                nc.vector.tensor_tensor(x1[:, k], twice, factor, ALU.mult).then_inc(s_x1, 1)
            low_part(NT - 1)

        @block.tensor
        def _(pe):
            pe.wait_ge(s_id, 1)
            for b in range(NP):
                for t in range(2 * b, 2 * b + 2):
                    pe.wait_ge(s_adj[t], 16)
                    if t >= 2:
                        pe.wait_ge(s_alo, t - 1)
                    for j in range(NT):
                        last = nc.tensor.transpose(adj_banks(t)[:, j, :], graph[:, t, j * P:(j + 1) * P], ident[:])
                    last.then_inc(s_tr, 1)
                pe.wait_ge(s_x[b], 32)
                if b >= 2:
                    pe.wait_ge(s_xtc, b - 1)
                for t in range(NT):
                    last = nc.tensor.transpose(x1_banks(b)[:, t, :], x0[:, t, b * P:(b + 1) * P], ident[:])
                last.then_inc(s_xtr, 1)
            pe.wait_ge(s_wbd, 8)
            pe.wait_ge(s_xtc, NP)
            pe.wait_ge(s_alo, NT)
            for t in range(NT):
                if t >= 2:
                    pe.wait_ge(s_ud, t - 1)
                for b in range(NP):
                    last = nc.tensor.matmul(bank[:, 4 * (t % 2) + b, 0:4 * C], xt[:, b, t * P:(t + 1) * P],
                                            wbd[:, 0:2].rearrange("p k b c -> p (k b c)"), start=True, stop=True)
                last.then_inc(s_u, 1)
            pe.wait_ge(s_ud, NT)

            def adj_product(t, hi, lo, fresh):
                for j in range(NT):
                    if fresh and j == 0:
                        pe.wait_ge(s_vlo, NT - 1)
                    if fresh and j == NT - 1:
                        pe.wait_ge(s_vlo, NT)
                    cols = slice(t * P, (t + 1) * P)
                    nc.tensor.matmul(bank[:, t % 2, :], adj_hi[:, j, cols], hi[:, j, :], start=(j == 0), stop=False)
                    if j == 0 and lo is u_lo:
                        for b in range(NP):
                            nc.tensor.matmul(bank[:, t % 2, b * P:(b + 1) * P], xt[:, b, cols],
                                             wbd[:, 2].rearrange("p b c -> p (b c)"), start=False, stop=False)
                    nc.tensor.matmul(bank[:, t % 2, :], adj_hi[:, j, cols], lo[:, j, :], start=False, stop=False)
                    last = nc.tensor.matmul(bank[:, t % 2, :], adj_lo[:, j, cols], hi[:, j, :], start=False,
                                            stop=(j == NT - 1))
                last.then_inc(s_av, 1)

            for t in range(NT):
                if t >= 2:
                    pe.wait_ge(s_vlo, t - 1)
                adj_product(t, u_hi, u_lo, False)
            pe.wait_ge(s_w, 64)
            for h in range(H):
                nc.tensor.transpose(bank[:, 4, h * C:(h + 1) * C], w_rows[:, h, :], ident[0:C, 0:C])
            nc.tensor.transpose(bank[:, 5, 0:H], bias_rows[:], ident[0:H, 0:H]).then_inc(s_wtr, 1)

            def turn_x1(t):
                pe.wait_ge(s_x1, t + 1)
                if t >= 2:
                    pe.wait_ge(s_lo, t - 1)
                for b in range(B):
                    last = nc.tensor.transpose(x1_banks(t)[:, b, :], x1[:, t % 2, b].rearrange("p k c -> p (k c)"),
                                               ident[:])
                last.then_inc(s_t1, 1)

            for t in range(NT):
                if t >= 2:
                    pe.wait_ge(s_r, t - 1)
                adj_product(t, v_hi, v_lo, t == 0)
                if t == 0:
                    pe.wait_ge(s_wtc, 2)
                    for h in range(H):
                        wt = w_t[:, h].rearrange("p k c -> p (k c)")
                        last = nc.tensor.matmul(m_bank[:, h // 2, h % 2, :], wt, w_t[:, h, 0, :], start=True,
                                                stop=True)
                    last.then_inc(s_m, 1)
                    pe.wait_ge(s_bad, 2 * NT + 5)
                    nc.tensor.transpose(bank[0:1, 2, 0:P], bad[:, 3:4], ident[:]).then_inc(s_badt, 1)
                if t >= 2:
                    turn_x1(t - 2)
            turn_x1(NT - 2)
            turn_x1(NT - 1)


def attention(nc, ctx, sem, env):
    wout, out = (env[k] for k in ("wout", "out"))
    B, N, C, H, D, NT, HT, JOBS1, JOBS = (env[k] for k in ("B", "N", "C", "H", "D", "NT", "HT", "JOBS1", "JOBS"))
    graph, x_hi, x_lo, m_table, m_now, ident, dup, sel, head_bias, out_bias, general, x1_dram, w_dram = (
        env[k] for k in ("graph", "x_hi", "x_lo", "m_table", "m_now", "ident", "dup", "sel", "head_bias",
                         "out_bias", "general", "x1_dram", "w_dram"))

    def sb(name, shape, dt=F32):
        return ctx.enter_context(nc.sbuf_tensor(name, shape, dt))

    def ps(name, shape):
        return ctx.enter_context(nc.psum_tensor(name, shape, F32))

    scores = ps("scores", [P, 2, N])
    turned = ps("turned", [P, NT, P])
    mixed = ps("mixed", [P, BANK])
    small = ps("small", [P, BANK])

    gated = sb("gated", [P, 2, N])
    prob = sb("prob", [P, 4, N])
    prob_t = sb("prob_t", [P, 2, NT, BANK])
    y_parts = sb("y_parts", [P, 2, N], F32R)
    x_rows = sb("x_rows", [P, 2, NT * C])
    bias_now = sb("bias_now", [P, 2, 2])
    w_now = sb("w_now", [P, 2, 2, D], F32R)
    wout_now = sb("wout_now", [P, 2, C])
    recip_b = sb("recip_b", [P, BANK])
    mixed_n = sb("mixed_n", [P, BANK])
    mixed_hi = sb("mixed_hi", [P, BANK], F32R)
    mixed_lo = sb("mixed_lo", [P, BANK], F32R)
    head_neg = sb("head_neg", [P, 2, BANK])
    head_act = sb("head_act", [P, 2, BANK])
    h_acc = sb("h_acc", [P, B, BANK])
    y_raw = sb("y_raw", [P, N])
    row_max = sb("row_max", [P, NT])
    neg_max = sb("neg_max", [P, NT])
    mask_at = sb("mask_at", [P, NT])
    row_sum = sb("row_sum", [P, 2, NT])
    recip = sb("recip", [P, 2, NT])
    fin, fin2 = (head_neg[:, k].rearrange("p (t c) -> p t c", c=C) for k in range(2))
    x1_b, y_out = (head_act[:, k].rearrange("p (t c) -> p t c", c=C) for k in range(2))
    h_now = m_table[:].rearrange("p h k c -> p (h k c)").bitcast(F32)
    stat = sb("fstat", [P, 4, NT])
    idle = sb("idle", [P, NT])
    consts = sb("consts", [P, 5, NT])

    s_scores = sem("scores_ready")
    s_gated = sem("gated_ready")
    s_shift = sem("shift_ready")
    s_exp = sem("exp_ready")
    s_prob = sem("prob_ready")
    s_turned = sem("turned_ready")
    s_prob_t = sem("prob_t_ready")
    s_mixed = sem("mixed_ready")
    s_recip = sem("recip_ready")
    s_rst = sem("recip_stored")
    s_rbc = [sem(f"recip_spread{a}") for a in range(2)]
    s_norm = sem("mixed_n_ready")
    s_nhi = sem("mixed_high_ready")
    s_nlo = sem("mixed_low_ready")
    s_post = sem("post_product_ready")
    s_raw = sem("head_split_ready")
    s_act = sem("head_act_ready")
    s_out1 = sem("wout_product_ready")
    s_acc = sem("h_acc_ready")
    s_zero = sem("h_acc_zeroed")
    s_y = sem("y_product_ready")
    s_yraw = sem("y_raw_ready")
    s_yhi = sem("y_high_ready")
    s_ylow = sem("y_low_ready")
    s_ylo = [sem(f"y_low_moved{k}") for k in range(2)]
    s_h = sem("h_product_ready")
    s_hhi = sem("h_high_ready")
    s_hlo = sem("h_low_ready")
    s_hsp = sem("h_parts_spread")
    s_hrow = sem("h_rows_product_ready")
    s_hrc = sem("h_rows_ready")
    s_fin = sem("fin_ready")
    s_fd = sem("final_steps_dve")
    s_fs = sem("final_sums")
    s_fp = sem("final_steps_pool")
    s_m = sem("m_loaded")
    s_xr = [sem(f"x_rows_loaded{k}") for k in range(2)]
    s_wl = [sem(f"w_loaded{k}") for k in range(2)]
    s_x1 = sem("x1_b_loaded")
    s_store = sem("out_stored")
    s_consts = sem("consts_ready")
    s_gen = sem("general_dve")

    def kind(n):
        return 0 if n < 0 or n >= JOBS else 1 if n < JOBS1 else 2

    def run(eng, body):
        def one(n):
            body(Job(n // 2, n % 2), kind(n + 1), kind(n), kind(n - 1), kind(n - 2))

        for n in range(2):
            one(n)
        with eng.Fori(1, JOBS1 // 2 - 1) as pair:
            for odd in range(2):
                body(Job(pair, odd), 1, 1, 1, 1)
        for n in range(JOBS1 - 2, JOBS1 + 2):
            one(n)
        with eng.Fori(JOBS1 // 2 + 1, JOBS // 2 - 1) as pair:
            for odd in range(2):
                body(Job(pair, odd), 2, 2, 2, 2)
        for n in range(JOBS - 2, JOBS + 2):
            one(n)

    def pair_ahead(job):
        return job.odd == 0 and not (isinstance(job.pair, int) and job.pair >= JOBS1 // 2 - 1)

    def own_rows(job):
        return slice(job.odd * C, (job.odd + 1) * C)

    def batch(job, k):
        return job.pair // (H // 2) if k == 1 else (job.pair - JOBS1 // 2) * 2 + job.odd

    def spread(row):
        return row.rearrange("p (t c) -> p t c", c=1).broadcast_to([P, NT, C])

    def head(job):
        return (job.pair % (H // 2)) * 2 + job.odd

    recip_dram = nc.dram_tensor("recip_scratch", [2, N], F32, kind="Internal").ap()
    block = ctx.enter_context(nc.Block())

    @block.sync
    def _(sp):
        def load_m(pair):
            sp.wait_ge(s_y, pair * 2)
            sp.dma_start(m_now[:].bitcast(F32),
                         m_table[:, pair % (H // 2)].bitcast(F32).rearrange("p k c -> p (k c)")).then_inc(s_m, 16)

        def move_low(job):
            sp.wait_ge(s_ylow, job.count(2, 2))
            other = slice((1 - job.odd) * C, (2 - job.odd) * C)
            sp.dma_start(y_parts[other, job.odd].bitcast(F32), y_raw[own_rows(job), :]).then_inc(s_ylo[job.odd], 16)

        def load_rows(job):
            wait(sp, s_mixed, job.count(2, -2))
            sp.dma_start(x_rows[:, job.odd], x1_dram[batch(job, 1)]).then_inc(s_xr[job.odd], 16)

        def load_weights(job):
            wait(sp, s_out1, job.count(1, -1))
            sp.dma_start(bias_now[:, job.odd], head_bias[:, head(job)]).then_inc(s_wl[job.odd], 16)
            for k in range(2):
                sp.dma_start(w_now[k * C:(k + 1) * C, job.odd].bitcast(F32), w_dram[head(job)]
                             ).then_inc(s_wl[job.odd], 16)
            sp.dma_start(wout_now[:, job.odd], wout.rearrange("(h d) c -> h d c", h=H)[head(job)]
                         ).then_inc(s_wl[job.odd], 16)

        def spread_recip(job, a):
            row = recip_dram[job.odd, a * BANK:(a + 1) * BANK]
            sp.wait_ge(s_recip, job.count(2, a + 1))
            with nc.allow_non_contiguous_dma(reason="512 numbers"):
                sp.dma_start(row.rearrange("(t p) -> p t", p=P), recip[:, job.odd, a * HT:(a + 1) * HT]
                             ).then_inc(s_rst, 16)
            sp.wait_ge(s_rst, job.count(32, 16 * a + 16))
            sp.dma_start(recip_b[:], row.rearrange("(k n) -> k n", k=1).broadcast_to([P, BANK])
                         ).then_inc(s_rbc[a], 16)

        def body(job, nxt, now, bef, bef2):
            if now == 1 and pair_ahead(job):
                load_m(job.pair + 1)
            if now == 1:
                load_rows(job)
            if bef:
                spread_recip(job.back(1), 0)
            if nxt == 1:
                move_low(job.back(-1))
            if now == 1:
                load_weights(job)
            if bef:
                spread_recip(job.back(1), 1)
            if bef2 == 2:
                j2 = job.back(2)
                b = batch(j2, 2)
                sp.wait_ge(s_fp, j2.count(5, 5 - 5 * JOBS1))
                sp.dma_start(out[b].rearrange("(t p) c -> p t c", p=P), y_out).then_inc(s_store, 16)
            if bef == 2:
                j1 = job.back(1)
                if isinstance(j1.pair, int) and j1.pair == JOBS1 // 2 and j1.odd == 0:
                    sp.wait_ge(s_out1, JOBS1)
                wait(sp, s_fp, j1.count(5, 0 - 5 * JOBS1))
                sp.dma_start(x1_b.rearrange("p t c -> p (t c)"), x1_dram[batch(j1, 2)]).then_inc(s_x1, 16)

        move_low(Job(0, 0))
        run(sp, body)
        sp.wait_ge(s_store, 16 * B)

    @block.tensor
    def _(pe):
        def y_product(pair, a):
            cols = slice(a * BANK, (a + 1) * BANK)
            b = pair // (H // 2)
            nc.tensor.matmul(small[:], m_now[:], x_hi[:, b, cols], start=True, stop=False)
            nc.tensor.matmul(small[:], m_now[:], x_lo[:, b, cols], start=False, stop=True).then_inc(s_y, 1)

        def h_product(job, a):
            b = batch(job, 2)
            pe.wait_ge(s_acc, b * H + H)
            nc.tensor.matmul(small[:], sel[:, a], h_acc[:, b], start=True, stop=True).then_inc(s_h, 1)

        def post_product(job, k, a):
            if k == 1:
                pe.wait_ge(s_nlo, job.count(2, a + 1))
                pe.wait_ge(s_wl[job.odd], job.pair * 64 + 64)
                nc.tensor.matmul(small[:], w_now[:, job.odd, 0], mixed_hi[:], start=True, stop=False)
                nc.tensor.matmul(small[:], w_now[:, job.odd, 0], mixed_lo[:], start=False, stop=False)
                nc.tensor.matmul(small[:], w_now[:, job.odd, 1], mixed_hi[:], start=False,
                                 stop=True).then_inc(s_post, 1)
            else:
                pe.wait_ge(s_norm, job.count(2, a + 1))
                for i in range(HT):
                    last = nc.tensor.matmul(small[:, i * C:(i + 1) * C], mixed_n[:, i * P:(i + 1) * P],
                                            dup[:], start=True, stop=True)
                last.then_inc(s_post, 1)

        def post_free(job, k, a):
            if k == 1:
                wait(pe, s_raw, job.count(2, a + 1))
            elif k == 2:
                pe.wait_ge(s_fin, job.count(2, a + 1 - 2 * JOBS1))

        def body(job, nxt, now, bef, bef2):
            j1, j2, jn = job.back(1), job.back(2), job.back(-1)

            def mix(t):
                a, pair = t // HT, t % HT
                if pair == 0:
                    pe.wait_ge(s_prob_t, j1.count(NT, a * HT + HT))
                    wait(pe, s_norm, j1.count(2, a))
                if t == 0:
                    if bef == 1:
                        pe.wait_ge(s_xr[j1.odd], j1.pair * 16 + 16)
                    else:
                        pe.wait_ge(s_hrc, j1.count(1, 1 - JOBS1))
                for e in range(2):
                    m = 2 * pair + e
                    last = nc.tensor.matmul(mixed[e * C:(e + 1) * C, :], x_rows[:, j1.odd, m * C:(m + 1) * C],
                                            prob_t[:, a, m, :], start=(pair == 0), stop=(pair == HT - 1))
                if pair == HT - 1:
                    last.then_inc(s_mixed, 1)

            for t in range(NT):
                if bef and t % HT == HT - 1:
                    mix(t)
                if now:
                    wait(pe, s_gated, job.count(NT, t - 1))
                    if t == 0 and now == 1:
                        pe.wait_ge(s_yhi, job.count(1, 1))
                        pe.wait_ge(s_ylo[job.odd], job.pair * 16 + 16)
                    if t == 0 and now == 2:
                        pe.wait_ge(s_hlo, job.count(2, 2 - 2 * JOBS1))
                        pe.wait_ge(s_hsp, job.count(4, 4 - 4 * JOBS1))
                    b = batch(job, now)
                    for a in range(2):
                        cols = slice(a * BANK, (a + 1) * BANK)
                        lhs = y_parts[:, job.odd, t * P:(t + 1) * P]
                        nc.tensor.matmul(scores[:, t % 2, cols], lhs, x_hi[:, b, cols], start=True, stop=False)
                        last = nc.tensor.matmul(scores[:, t % 2, cols], lhs, x_lo[:, b, cols], start=False, stop=True)
                    last.then_inc(s_scores, 1)
                if bef and 0 < t % HT < HT - 1:
                    mix(t)
                if (t >= 3 and now) or (t < 3 and bef):
                    pe.wait_ge(s_prob, job.count(NT, t - 2))
                    wait(pe, s_prob_t, job.count(NT, t - 3))
                    for m in range(NT):
                        last = nc.tensor.transpose(turned[:, m, :], prob[:, (t - 3) % 4, m * P:(m + 1) * P], ident[:])
                    last.then_inc(s_turned, 1)
                if t == 1 and bef2:
                    post_free(j2, bef2, 0)
                    post_product(j2, bef2, 1)
                if t == 3 and bef2 == 1:
                    pe.wait_ge(s_act, j2.count(2, 2))
                    for a in range(2):
                        last = nc.tensor.matmul(small[a * C:(a + 1) * C, :], wout_now[:, j2.odd], head_act[:, a],
                                                start=True, stop=True)
                    last.then_inc(s_out1, 1)
                if t == 3 and now == 2:
                    if bef2 == 1:
                        pe.wait_ge(s_acc, j2.count(1, 1))
                    else:
                        post_free(j2, bef2, 1)
                    for i in range(HT):
                        last = nc.tensor.transpose(small[:, i * P:(i + 1) * P], h_now[:, i * P:(i + 1) * P], ident[:])
                    last.then_inc(s_hrow, 1)
                if t == (4 if nxt == 2 else 5) and bef2 == 1:
                    pe.wait_ge(s_acc, j2.count(1, 1))
                if t in (5, 6) and now == 1 and pair_ahead(job):
                    if t == 5:
                        pe.wait_ge(s_m, job.pair * 16 + 16)
                    else:
                        pe.wait_ge(s_yraw, job.pair * 2 + 3)
                    y_product(job.pair + 1, t - 5)
                if t in (4, 5) and nxt == 2:
                    if t == 4 and now == 2:
                        pe.wait_ge(s_hrc, job.count(1, 1 - JOBS1))
                    wait(pe, s_hhi, jn.count(2, t - 4 - 2 * JOBS1))
                    h_product(jn, t - 4)
                if t == 7 and bef:
                    if now == 1 and pair_ahead(job):
                        pe.wait_ge(s_yraw, job.pair * 2 + 4)
                    elif nxt == 2:
                        pe.wait_ge(s_hhi, jn.count(2, 2 - 2 * JOBS1))
                    elif nxt == 0:
                        post_free(j2, bef2, 1)
                        if now == 2:
                            pe.wait_ge(s_hrc, job.count(1, 1 - JOBS1))
                    post_product(j1, bef, 0)
                if bef and t % HT == 0:
                    mix(t)

        y_product(0, 0)
        pe.wait_ge(s_yraw, 1)
        y_product(0, 1)
        run(pe, body)

    @block.scalar
    def _(act):
        def y_copy(pair, a):
            act.wait_ge(s_y, pair * 2 + (a + 1))
            nc.scalar.activation(y_raw[:, a * BANK:(a + 1) * BANK], small[:], ACT.Copy).then_inc(s_yraw, 1)

        def y_high(job):
            rows = own_rows(job)
            act.wait_ge(s_yraw, job.pair * 2 + 2)
            nc.scalar.activation(y_parts[rows, job.odd], y_raw[rows, :], ACT.Copy).then_inc(s_yhi, 1)

        def h_high(job, a):
            cols = slice(a * BANK, (a + 1) * BANK)
            act.wait_ge(s_h, job.count(2, a + 1 - 2 * JOBS1))
            wait(act, s_hrow, job.count(1, -JOBS1))
            rows = slice(a * C, (a + 1) * C)
            nc.scalar.activation(h_now[rows, :], small[rows, :], ACT.Copy)
            nc.scalar.activation(y_parts[:, job.odd, cols], small[:], ACT.Copy)
            if isinstance(job.pair, int) and job.pair == JOBS1 // 2 and job.odd == 0:
                act.wait_ge(s_ylo[1], JOBS1 // 2 * 16)
            wait(act, s_hlo, job.count(2, a - 1 - 2 * JOBS1))
            nc.scalar.activation(y_raw[:, cols], small[:], ACT.Copy).then_inc(s_hhi, 1)

        def mixed_high(job, a):
            act.wait_ge(s_norm, job.count(2, a + 1))
            wait(act, s_post, job.count(2, a))
            nc.scalar.activation(mixed_hi[:], mixed_n[:], ACT.Copy).then_inc(s_nhi, 1)

        def head_out(job, a):
            act.wait_ge(s_post, job.count(2, a + 1))
            wait(act, s_out1, job.count(1, 0))
            nc.scalar.activation(head_act[:, a], small[:], ACT.Relu, bias=bias_now[:, job.odd, 0:1], scale=1.0)
            nc.scalar.activation(head_neg[:, a], small[:], ACT.Relu, bias=bias_now[:, job.odd, 1:2],
                                 scale=-SLOPE).then_inc(s_raw, 1)

        def body(job, nxt, now, bef, bef2):
            j1, j2, jn = job.back(1), job.back(2), job.back(-1)
            for t in range(NT):
                if (t >= 1 and now) or (t < 1 and bef):
                    act.wait_ge(s_shift, job.count(NT, t))
                    wait(act, s_turned, job.count(NT, t - 4))
                    k = (t - 1) % NT
                    nc.scalar.activation(prob[:, k % 4], gated[:, k % 2], ACT.Exp, bias=neg_max[:, k:k + 1],
                                         scale=1.0).then_inc(s_exp, 1)
                if (t >= 3 and now) or (t < 3 and bef):
                    k = (t - 3) % NT
                    act.wait_ge(s_turned, job.count(NT, t - 2))
                    if k % HT == 0:
                        wait(act, s_mixed, (job if t >= 3 else j1).count(2, k // HT - 1))
                    nc.scalar.activation(prob_t[:, k // HT, :, (k % HT) * P:(k % HT + 1) * P], turned[:],
                                         ACT.Copy).then_inc(s_prob_t, 1)
                if t == 1 and bef2 == 1:
                    head_out(j2, 1)
                if t == 3 and now == 2:
                    act.wait_ge(s_hrow, job.count(1, 1 - JOBS1))
                    act.wait_ge(s_mixed, job.count(2, -2))
                    nc.scalar.activation(x_rows[:, job.odd].rearrange("p (a i c) -> p i a c", a=2, c=C),
                                         small[:].rearrange("p (i a c) -> p i a c", a=2, c=C),
                                         ACT.Copy).then_inc(s_hrc, 1)
                if t == 0 and bef2 == 1:
                    mixed_high(j2, 1)
                if t == 4 and bef == 1:
                    mixed_high(j1, 0)
                if t in (5, 6) and now == 1 and pair_ahead(job):
                    if t == 5:
                        act.wait_ge(s_ylo[1], job.pair * 16 + 16)
                    y_copy(job.pair + 1, t - 5)
                if t == 1 and nxt == 1:
                    y_high(jn)
                if t in (4, 5) and nxt == 2:
                    h_high(jn, t - 4)
                if t == 7 and bef == 1:
                    head_out(j1, 0)

        for a in range(2):
            y_copy(0, a)
        y_high(Job(0, 0))
        run(act, body)

    @block.gpsimd
    def _(pool):
        nc.gpsimd.memset(h_acc[:], 0.0).then_inc(s_zero, 1)
        for k, value in enumerate((-1.0, -0.5, -1.0 / C, 1.0 / C, EPS)):
            nc.gpsimd.memset(consts[:, k], value).then_inc(s_consts, 1)
        pool.wait_ge(s_consts, 5)

        def y_low(job, a, shifts, acts):
            rows, cols = own_rows(job), slice(a * BANK, (a + 1) * BANK)
            pool.wait_ge(s_yhi, job.count(1, 1))
            wait(pool, s_shift, shifts)
            wait(pool, s_act, acts)
            nc.gpsimd.tensor_tensor(y_raw[rows, cols], y_raw[rows, cols], y_parts[rows, job.odd, cols].bitcast(F32),
                                    ALU.subtract).then_inc(s_ylow, 1)
            pool.wait_ge(s_ylow, job.count(2, a + 1))

        def h_low(job, a, shifts):
            cols = slice(a * BANK, (a + 1) * BANK)
            pool.wait_ge(s_hsp, job.count(4, 2 * a + 2 - 4 * JOBS1))
            pool.wait_ge(s_shift, shifts)
            nc.gpsimd.tensor_tensor(y_parts[C:P, job.odd, cols], y_raw[C:P, cols],
                                    y_parts[C:P, job.odd, cols].bitcast(F32), ALU.subtract).then_inc(s_hlo, 1)
            pool.wait_ge(s_hlo, job.count(2, a + 1 - 2 * JOBS1))

        def mixed_low(job, a):
            pool.wait_ge(s_nhi, job.count(2, a + 1))
            nc.gpsimd.tensor_tensor(mixed_lo[:], mixed_n[:], mixed_hi[:].bitcast(F32),
                                    ALU.subtract).then_inc(s_nlo, 1)

        def leaky(job, a):
            pool.wait_ge(s_raw, job.count(2, a + 1))
            nc.gpsimd.tensor_tensor(head_act[:, a], head_act[:, a], head_neg[:, a], ALU.subtract).then_inc(s_act, 1)

        def final_step(job, part):
            n = job.count(1, -JOBS1)
            if part == 0:
                pool.wait_ge(s_fs, n * 2 + 1)
                nc.gpsimd.tensor_tensor(stat[:, 1], stat[:, 0], consts[:, 2], ALU.mult).then_inc(s_fp, 1)
            elif part == 1:
                pool.wait_ge(s_fs, n * 2 + 2)
                nc.gpsimd.tensor_tensor(stat[:, 3], stat[:, 2], consts[:, 3], ALU.mult).then_inc(s_fp, 1)
                pool.wait_ge(s_fp, n * 5 + 2)
                nc.gpsimd.tensor_tensor(stat[:, 3], stat[:, 3], consts[:, 4], ALU.add).then_inc(s_fp, 1)
                pool.wait_ge(s_fp, n * 5 + 3)
                nc.gpsimd.tensor_tensor(stat[:, 3], stat[:, 3], consts[:, 1], ALU.pow).then_inc(s_fp, 1)
            else:
                pool.wait_ge(s_fp, n * 5 + 4)
                nc.gpsimd.tensor_tensor(y_out, fin2, spread(stat[:, 3]), ALU.mult).then_inc(s_fp, 1)

        def body(job, nxt, now, bef, bef2):
            j1, j2, jn = job.back(1), job.back(2), job.back(-1)
            for t in range(NT):
                if bef2 == 2 and t == 4:
                    final_step(j2, 0)
                if now:
                    pool.wait_ge(s_gated, job.count(NT, t + 1))
                    nc.gpsimd.tensor_tensor(neg_max[:, t:t + 1], row_max[:, t:t + 1], consts[:, 0, 0:1], ALU.mult)
                    nc.gpsimd.tensor_scalar(mask_at[:, t:t + 1], row_max[:, t:t + 1], 0.0, NEVER, ALU.is_le,
                                            ALU.mult).then_inc(s_shift, 1)
                if t == 0 and bef2 == 1:
                    mixed_low(j2, 1)
                if t == 2 and bef2 == 1:
                    leaky(j2, 1)
                if t in (2, 3) and nxt == 1:
                    y_low(jn, t - 2, job.count(NT, t + 1), j2.count(2, 2))
                if t in (4, 5) and nxt == 2:
                    h_low(jn, t - 4, job.count(NT, t + 1))
                if t == 4 and bef == 1:
                    mixed_low(j1, 0)
                if t == 7 and bef == 1:
                    leaky(j1, 0)
                if bef2 == 2 and t in (6, 7):
                    final_step(j2, t - 5)

        for a in range(2):
            y_low(Job(0, 0), a, 0, 0)
        run(pool, body)

    @block.vector
    def _(dve):
        def h_parts(job, a):
            cols = slice(a * BANK, (a + 1) * BANK)
            dve.wait_ge(s_hhi, job.count(2, a + 1 - 2 * JOBS1))
            nc.vector.tensor_scalar(x_hi[:, batch(job, 2), cols], y_parts[:, job.odd, cols].bitcast(F32), 1.0, None,
                                    ALU.mult).then_inc(s_hsp, 1)
            nc.vector.tensor_tensor(x_lo[:, batch(job, 2), cols], y_raw[:, cols],
                                    y_parts[:, job.odd, cols].bitcast(F32), ALU.subtract).then_inc(s_hsp, 1)

        def reciprocals(job, a):
            dve.wait_ge(s_prob, job.count(NT, a * HT + HT))
            cols = slice(a * HT, (a + 1) * HT)
            nc.vector.reciprocal(recip[:, job.odd, cols], row_sum[:, job.odd, cols]).then_inc(s_recip, 1)

        def normalise(job, a):
            dve.wait_ge(s_mixed, job.count(2, a + 1))
            dve.wait_ge(s_rbc[a], job.count(16, 16))
            wait(dve, s_post, job.count(2, a))
            nc.vector.tensor_tensor(mixed_n[:], mixed[:], recip_b[:], ALU.mult).then_inc(s_norm, 1)

        def accumulate(job):
            dve.wait_ge(s_out1, job.count(1, 1))
            wait(dve, s_acc, job.count(1, 0))
            b = batch(job, 1)
            nc.vector.tensor_tensor(h_acc[:, b], small[:], h_acc[:, b], ALU.add).then_inc(s_acc, 1)

        def final_rows(job, a):
            dve.wait_ge(s_post, job.count(2, a + 1))
            if isinstance(job.pair, int):
                wait(dve, s_fd, job.count(4, 1 - 4 * JOBS1 - 4))
            else:
                dve.wait_ge(s_gated, job.count(NT, 2 * NT))
            nc.vector.tensor_tensor(fin[:, a * HT:(a + 1) * HT, :],
                                    small[:, 0:HT * C].rearrange("p (t c) -> p t c", c=C),
                                    out_bias[:].rearrange("p (a c) -> p a c", a=1).broadcast_to([P, HT, C]),
                                    ALU.add).then_inc(s_fin, 1)

        def final_step(job, part):
            n = job.count(1, -JOBS1)
            if part == 0:
                dve.wait_ge(s_fin, n * 2 + 2)
                wait(dve, s_fp, n * 5)
                nc.vector.scalar_tensor_tensor(out=fin2, in0=fin, scalar=SLOPE, in1=fin, op0=ALU.mult,
                                               op1=ALU.max).then_inc(s_fd, 1)
                dve.wait_ge(s_fd, n * 4 + 1)
                dve.wait_ge(s_x1, n * 16 + 16)
                nc.vector.tensor_tensor(fin2, fin2, x1_b, ALU.add).then_inc(s_fd, 1)
            elif part == 1:
                dve.wait_ge(s_fd, n * 4 + 2)
                nc.vector.reduce_sum(stat[:, 0], fin2, AX_X).then_inc(s_fs, 1)
            elif part == 2:
                dve.wait_ge(s_fp, n * 5 + 1)
                nc.vector.tensor_tensor(fin2, fin2, spread(stat[:, 1]), ALU.add).then_inc(s_fd, 1)
            else:
                dve.wait_ge(s_fd, n * 4 + 3)
                wait(dve, s_store, n * 16)
                nc.vector.tensor_tensor(y_out, fin2, fin2, ALU.mult).then_inc(s_fd, 1)
                dve.wait_ge(s_fd, n * 4 + 4)
                nc.vector.reduce_sum(stat[:, 2], y_out, AX_X).then_inc(s_fs, 1)

        def pipeline(general_graph):
            def body(job, nxt, now, bef, bef2):
                j1, j2, jn = job.back(1), job.back(2), job.back(-1)
                for t in range(NT):
                    if t == 1 and bef:
                        reciprocals(j1, 0)
                    if t == 5 and bef:
                        reciprocals(j1, 1)
                    if (t >= 2 and now) or (t < 2 and bef):
                        k = (t - 2) % NT
                        dve.wait_ge(s_exp, job.count(NT, t - 1))
                        nc.vector.scalar_tensor_tensor(
                            out=prob[:, k % 4], in0=gated[:, k % 2], scalar=mask_at[:, k:k + 1], in1=prob[:, k % 4],
                            op0=ALU.not_equal, op1=ALU.mult,
                            accum_out=row_sum[:, (job if t >= 2 else j1).odd, k:k + 1]).then_inc(s_prob, 1)
                    if t == 0 and bef2:
                        normalise(j2, 1)
                    if t == 0 and bef2 == 2:
                        final_rows(j2, 0)
                    if t == 2 and bef2 == 2:
                        final_rows(j2, 1)
                    if t in (3, 4, 5, 6) and bef2 == 2:
                        final_step(j2, t - 3)
                    if t == (4 if nxt == 2 else 5) and bef2 == 1:
                        accumulate(j2)
                    if t == 4 and bef:
                        normalise(j1, 0)
                    if t in (5, 6) and nxt == 2:
                        h_parts(jn, t - 5)
                    if now:
                        n = job.count(2 * NT, 2 * t)
                        dve.wait_ge(s_scores, job.count(NT, t + 1))
                        wait(dve, s_prob, job.count(NT, t - 1))
                        nc.vector.memset(idle[:, t:t + 1], 0.0)
                        ins = nc.vector.tensor_tensor_reduce(
                            out=gated[:, t % 2], in0=scores[:, t % 2], in1=graph[:, t], scale=1.0, scalar=LOWEST,
                            op0=ALU.mult, op1=ALU.max, accum_out=row_max[:, t:t + 1])
                        if not general_graph:
                            ins.then_inc(s_gated, 1)
                        else:
                            ins.then_inc(s_gen, 1)
                            dve.wait_ge(s_gen, n + 1)
                            zeros = prob[:, t % 4]
                            nc.vector.tensor_scalar(zeros, gated[:, t % 2], 0.0, NEG_INF, ALU.is_equal,
                                                    ALU.mult).then_inc(s_gen, 1)
                            dve.wait_ge(s_gen, n + 2)
                            nc.vector.memset(idle[:, t:t + 1], 0.0)
                            nc.vector.tensor_tensor_reduce(
                                out=gated[:, t % 2], in0=gated[:, t % 2], in1=zeros, scale=1.0, scalar=LOWEST,
                                op0=ALU.add, op1=ALU.max, accum_out=row_max[:, t:t + 1]).then_inc(s_gated, 1)

            run(dve, body)

        dve.wait_ge(s_zero, 1)
        flag = dve.value_load(general[0:1, 0:1], min_val=0, max_val=1)
        with dve.If(flag == 0):
            pipeline(False)
        with dve.Else():
            pipeline(True)


_INS = ['x', 'adj', 'L0_gnn_weight', 'L0_gnn_bias', 'L1_gnn_Wh', 'L1_gnn_bh', 'L1_gnn_W_out', 'L1_gnn_b_out']


def kernel(**inputs):
    import numpy as _np
    import concourse.bacc as _bacc
    from concourse import mybir as _mybir
    from concourse.bass_utils import run_bass_kernel_spmd as _run

    nc = _bacc.Bacc("TRN2", target_bir_lowering=False, num_devices=1)
    arrays, args = {}, []
    for name in _INS:
        a = _np.ascontiguousarray(inputs[name])
        arrays[f"in_{name}"] = a
        args.append(nc.dram_tensor(f"in_{name}", a.shape, _mybir.dt.from_np(a.dtype), kind="ExternalInput").ap())
    args.append(nc.dram_tensor("out_0", inputs['x'].shape, _mybir.dt.float32, kind="ExternalOutput").ap())
    program(nc, *args)
    r = _run(nc, [arrays], core_ids=[0])
    return r.results[0]["out_0"]
```
